# Optimizing a Trainium2 kernel written in Bass

```python
import numpy as np
import jax
import jax.numpy as jnp

def _softmax(x, axis=-1):
    return jax.nn.softmax(x, axis=axis)

def _gelu(x):
    return jax.nn.gelu(x, approximate=True)

def _silu(x):
    return jax.nn.silu(x)

def _sigmoid(x):
    return jax.nn.sigmoid(x)

def _layernorm(x, axis=-1, eps=1e-05):
    m = jnp.mean(x, axis=axis, keepdims=True)
    v = jnp.var(x, axis=axis, keepdims=True)
    return (x - m) / jnp.sqrt(v + eps)

def _scatter_add(tgt, idx, src, axis=0):
    return tgt.at[idx].add(src)

def _segment_sum(src, seg, n):
    return jax.ops.segment_sum(src, seg, n)
kernel_name = 'mk_audio_tower_d1_tok_audfeat512_r4_4d97aa'

def setup_inputs(seed: int=0):
    np.random.seed(seed)
    _w = jnp.asarray

    def _rec_inputs():
        import jax
        import jax.numpy as jnp
        _rk = jax.random.key(seed)
        x = -0.00190633 + 1.00279 * jax.random.normal(jax.random.fold_in(_rk, 1), (16, 750, 7), jnp.float32)
        return x
    x = _rec_inputs()

    def _L0_tok_setup():
        import jax, jax.numpy as jnp
        import numpy as np
        SIG_DEPTH = 4

        def _outer(a, b):
            return (a[:, :, None] * b[:, None, :]).reshape(a.shape[0], -1)
        key = jax.random.key(seed)
        k1, k2 = jax.random.split(key)
        B, L, Cin = (64, 64, 7)
        out_dim = 128
        C = Cin + 1
        sig_channels = sum((C ** k for k in range(1, SIG_DEPTH + 1)))
        inp = jax.random.normal(k1, (B, L, Cin), dtype=jnp.float32)
        W = jax.random.normal(k2, (out_dim, sig_channels), dtype=jnp.float32) * 0.02
        b = jnp.zeros((out_dim,), dtype=jnp.float32)
        return {'inp': inp, 'W': W, 'b': b}
    _L0_tok_all = _L0_tok_setup()
    _L0_tok_in = {k: v for k, v in _L0_tok_all.items() if k in ('W', 'b')}
    del _L0_tok_all

    def _L0_attn_setup():
        import jax, jax.numpy as jnp
        import numpy as np
        B, N_CTX, D_MODEL = (2, 1024, 128)
        key = jax.random.key(seed)
        kx, kw = jax.random.split(key)
        x = jax.random.normal(kx, (B, N_CTX, D_MODEL), dtype=jnp.float32)
        W = jax.random.normal(kw, (D_MODEL, D_MODEL), dtype=jnp.float32) * 0.02
        return {'x': x, 'W': W}
    _L0_attn_all = _L0_attn_setup()
    _L0_attn_in = {k: v for k, v in _L0_attn_all.items() if k in ('W',)}
    del _L0_attn_all

    def _L0_ffn_setup():
        import jax, jax.numpy as jnp
        import numpy as np
        from jax import lax
        N_EXPERTS = 16
        TOP_K = 2
        D_MODEL = 128
        D_FF = 512
        key = jax.random.key(seed)
        ks = jax.random.split(key, 7)
        s_in = 1.0 / np.sqrt(D_MODEL)
        s_ff = 1.0 / np.sqrt(D_FF)
        x = jax.random.normal(ks[0], (2, 512, D_MODEL), dtype=jnp.float32)
        router_w = jax.random.uniform(ks[1], (N_EXPERTS, D_MODEL), jnp.float32, -s_in, s_in)
        router_b = jax.random.uniform(ks[2], (N_EXPERTS,), jnp.float32, -s_in, s_in)
        w1 = jax.random.uniform(ks[3], (N_EXPERTS, D_FF, D_MODEL), jnp.float32, -s_in, s_in)
        b1 = jax.random.uniform(ks[4], (N_EXPERTS, D_FF), jnp.float32, -s_in, s_in)
        w2 = jax.random.uniform(ks[5], (N_EXPERTS, D_MODEL, D_FF), jnp.float32, -s_ff, s_ff)
        b2 = jax.random.uniform(ks[6], (N_EXPERTS, D_MODEL), jnp.float32, -s_ff, s_ff)
        return {'x': x, 'router_w': router_w, 'router_b': router_b, 'w1': w1, 'b1': b1, 'w2': w2, 'b2': b2}
    _L0_ffn_all = _L0_ffn_setup()
    _L0_ffn_in = {k: v for k, v in _L0_ffn_all.items() if k in ('router_w', 'router_b', 'w1', 'b1', 'w2', 'b2')}
    del _L0_ffn_all
    return {'x': x, 'L0_tok_W': _L0_tok_in['W'], 'L0_tok_b': _L0_tok_in['b'], 'L0_attn_W': _L0_attn_in['W'], 'L0_ffn_router_w': _L0_ffn_in['router_w'], 'L0_ffn_router_b': _L0_ffn_in['router_b'], 'L0_ffn_w1': _L0_ffn_in['w1'], 'L0_ffn_b1': _L0_ffn_in['b1'], 'L0_ffn_w2': _L0_ffn_in['w2'], 'L0_ffn_b2': _L0_ffn_in['b2']}

def reference(x, L0_tok_W, L0_tok_b, L0_attn_W, L0_ffn_router_w, L0_ffn_router_b, L0_ffn_w1, L0_ffn_b1, L0_ffn_w2, L0_ffn_b2):
    import jax
    import jax.numpy as jnp

    def _L0_tok_ref(inp, W, b):
        import jax, jax.numpy as jnp
        import numpy as np
        SIG_DEPTH = 4

        def _outer(a, b):
            return (a[:, :, None] * b[:, None, :]).reshape(a.shape[0], -1)
        B, L, Cin = inp.shape
        t = jnp.broadcast_to(jnp.linspace(0.0, 1.0, L, dtype=inp.dtype)[None, :, None], (B, L, 1))
        x = jnp.concatenate([t, inp], axis=-1)
        C = Cin + 1
        d = SIG_DEPTH
        dx = jnp.transpose(x[:, 1:] - x[:, :-1], (1, 0, 2))
        init = tuple((jnp.zeros((B, C ** (k + 1)), x.dtype) for k in range(d)))

        def step(levels, v):
            e = [v]
            for k in range(1, d):
                e.append(_outer(e[-1], v) / (k + 1))
            new = []
            for k in range(d):
                acc = levels[k] + e[k]
                for i in range(k):
                    acc = acc + _outer(levels[i], e[k - 1 - i])
                new.append(acc)
            sig = jnp.concatenate(new, axis=-1)
            return (tuple(new), sig)
        _, sigs = jax.lax.scan(step, init, dx)
        sigs = jnp.transpose(sigs, (1, 0, 2))
        return sigs @ W.T + b

    def _L0_attn_ref(x, W):
        import jax, jax.numpy as jnp
        import numpy as np
        B, N_CTX, D_MODEL = (2, 1024, 128)
        n_ctx = x.shape[-2]
        K = jnp.einsum('bnd,ed->bne', x, W)
        causal = jnp.tril(jnp.ones((n_ctx, n_ctx), dtype=bool))
        mask = jnp.where(causal, 0.0, -jnp.inf).astype(x.dtype)
        scores = jnp.einsum('bqd,bkd->bqk', x, K) + mask
        attn = jax.nn.softmax(scores, axis=-1)
        return x + jnp.einsum('bqk,bkd->bqd', attn, K)

    def _L0_ffn_ref(x, router_w, router_b, w1, b1, w2, b2):
        import jax, jax.numpy as jnp
        import numpy as np
        from jax import lax
        N_EXPERTS = 16
        TOP_K = 2
        D_MODEL = 128
        D_FF = 512
        B, S, D = x.shape
        xt = x.reshape(-1, D)
        logits = xt @ router_w.T + router_b
        probs = jax.nn.softmax(logits, axis=-1)
        topk_p, topk_i = lax.top_k(probs, TOP_K)
        onehot = jax.nn.one_hot(topk_i, N_EXPERTS, dtype=probs.dtype)
        gates = jnp.sum(onehot * topk_p[..., None], axis=1)

        def expert_step(acc, packed):
            w1e, b1e, w2e, b2e, ge = packed
            h = jax.nn.gelu(xt @ w1e.T + b1e, approximate=False)
            y = h @ w2e.T + b2e
            return (acc + y * ge[:, None], None)
        out, _ = lax.scan(expert_step, jnp.zeros_like(xt), (w1, b1, w2, b2, gates.T))
        return out.reshape(B, S, D)
    h = _L0_tok_ref(x, L0_tok_W, L0_tok_b)
    h = h + _L0_attn_ref(_layernorm(h, axis=-1), L0_attn_W)
    h = h + _L0_ffn_ref(_layernorm(h, axis=-1), L0_ffn_router_w, L0_ffn_router_b, L0_ffn_w1, L0_ffn_b1, L0_ffn_w2, L0_ffn_b2)
    return h

_drawn_inputs = setup_inputs


def setup_inputs(seed=0):
    import zlib

    import numpy as np

    out = dict(_drawn_inputs(seed))
    spreads = {'L0_tok_b': (0.0, 2.0)}
    factors = {'L0_attn_W': 28.224,
     'L0_ffn_router_w': 8.0,
     'L0_ffn_router_b': 28.837,
     'L0_ffn_w1': 8.0,
     'L0_ffn_b1': 60.585,
     'L0_ffn_w2': 8.0,
     'L0_ffn_b2': 200.0}
    for name, (base, spread) in spreads.items():
        noise = np.random.default_rng([zlib.crc32(name.encode()), seed]).standard_normal(out[name].shape)
        drawn = base * np.exp(spread * noise) if base else spread * noise
        out[name] = jnp.asarray(drawn.astype(out[name].dtype))
    for name, factor in factors.items():
        out[name] = (out[name] * factor).astype(out[name].dtype)
    return out
```

```python
from contextlib import ExitStack

import concourse.bass as bass
from concourse import mybir

F32 = mybir.dt.float32
F32R = mybir.dt.float32r
BF16 = mybir.dt.bfloat16
U32 = mybir.dt.uint32
ALU = mybir.AluOpType
ACT = mybir.ActivationFunctionType
AX = mybir.AxisListType

P = 128
B = 16
STEPS = 749
T = 6
LAST = STEPS - (T - 1) * P
C = 8
D = 128
E = 16
FF = 512
LH = 4
EPS = 1e-5
MASKED = -1e30
MAGIC = float(0x5F3759DF)
GROUPS = [[0, 1, 2], [3], [4], [5]]
PLACE = {0: 0, 2: P, 1: 4 * P, 3: 0, 4: 0, 5: 0}


def after(eng, sem, value):
    if not isinstance(value, int) or value > 0:
        eng.wait_ge(sem, value)


class Link:

    def __init__(self, eng, sem, base, per):
        self.eng, self.sem, self.base, self.per, self.n = eng, sem, base, per, 0

    def __call__(self, instruction):
        self.n += 1
        instruction.then_inc(self.sem, 1)
        self.eng.wait_ge(self.sem, self.base + self.n)

    def end(self):
        assert self.n == self.per, (self.n, self.per)


def build(nc, xa, xb, x0, w4, w3x, w3y, tok_b, attn_w, router_w, router_b, w1, b1, w2, b2, out):
    ctx = ExitStack()
    with ctx:
        def sb(name, shape, dt=F32):
            return ctx.enter_context(nc.sbuf_tensor(name, shape, dt))

        def sem(name):
            return ctx.enter_context(nc.semaphore(name))

        BT = B * T
        ident = sb("ident", [P, P])
        ones = sb("ones", [P, P])
        before = sb("before", [P, P + 1])
        upto = sb("upto", [P, P])
        ident16 = sb("ident16", [P, P], BF16)
        future = sb("future", [P, P], BF16)
        wstage = sb("wstage", [P, 2, 1024])
        w4h = sb("w4h", [P, 6, 1024], F32R)
        w4l = sb("w4l", [P, 6, 1024], F32R)
        waT = sb("waT", [P, D])
        rwT = sb("rwT", [P, E])
        rb = sb("rb", [P, E])
        bias0 = sb("bias0", [P, D])
        iota16 = sb("iota16", [P, T, E])
        iotai = sb("iotai", [P, T, E], mybir.dt.int32)
        NB1 = B + 1
        xas = sb("xas", [P, B * T * C])
        xbs = sb("xbs", [P, B * T * C])
        x0s = sb("x0s", [P, B * C])
        v_all = sb("v_all", [P, NB1 * T * C])
        a1_all = sb("a1_all", [P, NB1 * T * C])
        b1_all = sb("b1_all", [P, NB1 * T * C])
        d1_all = sb("d1_all", [P, NB1 * T * C])
        
        v_cur = sb("v_cur", [P, T, C])
        v_nxt = sb("v_nxt", [P, T, C])
        inc2 = sb("inc2", [P, T, 64])
        run2 = sb("run2", [P, T, 64])
        t1 = sb("t1", [P, T, 64])
        t2 = sb("t2", [P, T, 64])
        a2 = sb("a2", [P, T, 64])
        c2 = sb("c2", [P, T, 64])
        pack = sb("pack", [P, T, 256])
        inc3 = sb("inc3", [P, 2, 512])
        loc3 = sb("loc3", [P, 2, 512])
        carry = sb("carry", [P, T + 1, 4])
        a3h = sb("a3h", [P, 2, 512], F32R)
        a3l = sb("a3l", [P, 2, 512], F32R)
        packT = sb("packT", [P, 2, 256], F32R)
        dy = sb("dy", [P, 2, D])
        rundy = sb("rundy", [P, 2, D])
        hb = sb("hb", [P, T, D])
        h1 = sb("h1", [P, T, D])
        x1 = sb("x1", [P, T, D])
        x1T = sb("x1T", [P, T * P])
        kT = sb("kT", [P, T * P])
        kk = sb("kk", [P, T, D])
        negmax = sb("negmax", [P, T])
        rowsum = sb("rowsum", [P, T])
        rinv = sb("rinv", [P, T])
        probs = sb("probs", [P, T * P])
        probsT = sb("probsT", [P, T * P])
        st1 = sb("st1", [P, T, 6])
        st2 = sb("st2", [P, T, 6])
        nw = sb("nw", [P, 8, T])
        x2 = sb("x2", [P, T, D])
        x2T = sb("x2T", [P, T * P])
        lg = sb("lg", [P, T, E])
        pr = sb("pr", [P, T, E])
        sel = sb("sel", [P, 3, T, E])
        r6 = sb("r6", [P, 6, T])
        h_all = sb("h_all", [P, BT, D])
        x2T_all = nc.dram_tensor("x2T_all", [P, BT * P], F32).ap()
        x2T_blk = loc3
        xl = [sem("x2T_a"), sem("x2T_b")]
        gates = sb("gates", [P, BT, E])
        w1s = inc3[:, 0, :]
        w2s = inc3[:, 1, :].rearrange("p (c d) -> p c d", d=D)
        b1s = sb("b1s", [P, FF // P])
        b2s = rundy[:, 1, :]
        hT = [x[:, 0:512] for x in (x1T, kT, probs, probsT)]
        yb = rundy[:, 0, :]

        psP = ctx.enter_context(nc.psum_tensor("psP", [P, 2, 512], F32))
        psA = ctx.enter_context(nc.psum_tensor("psA", [P, 2, 512], F32))
        psS = ctx.enter_context(nc.psum_tensor("psS", [P, 512], F32))
        psO = ctx.enter_context(nc.psum_tensor("psO", [P, 512], F32))
        psW = ctx.enter_context(nc.psum_tensor("psW", [P, 1024], F32))

        ld = sem("loaded_small")
        ldw = [sem("loaded_w_a"), sem("loaded_w_b")]
        w_split = sem("w_split")
        w_hi = sem("w_hi")
        consts = sem("consts")
        pchain = sem("pool_chain")
        paths = sem("paths")
        inc2_ready, run2_ready, s2_sum = sem("inc2_ready"), sem("run2_ready"), sem("s2_sum")
        a2_ready = sem("a2_ready")
        inc3_ready, loc3_ready = sem("inc3_ready"), sem("loc3_ready")
        a3_sum, a3_hi, a3_lo = sem("a3_sum"), sem("a3_hi"), sem("a3_lo")
        pack_sum, pack_copied = sem("pack_sum"), sem("pack_copied")
        main_done, weighted = sem("main_done"), sem("weighted")
        rundy_ready, path_sum, h_ready = sem("rundy_ready"), sem("path_sum"), sem("h_ready")
        ch_pre, ch_w, ch_run2, ch_setup = sem("ch_pre"), sem("ch_w"), sem("ch_run2"), sem("ch_setup")
        h_saved, x1_ready, x1T_psum, x1T_ready = sem("h_saved"), sem("x1_ready"), sem("x1T_psum"), sem("x1T_ready")
        k_psum, k_ready, k_ready2 = sem("k_psum"), sem("k_ready"), sem("k_ready2")
        scores, negmax_ready, exp_ready = sem("scores"), sem("negmax_ready"), sem("exp_ready")
        pT_psum, pT_ready, pv_psum, attended = sem("pT_psum"), sem("pT_ready"), sem("pv_psum"), sem("attended")
        ch_ln1, ch_ln2, ch_att = sem("ch_ln1"), sem("ch_ln2"), sem("ch_att")
        x2_ready, x2T_psum, x2T_ready, logits = sem("x2_ready"), sem("x2T_psum"), sem("x2T_ready"), sem("logits")
        lg_ready, pr_ready, gates_ready = sem("lg_ready"), sem("pr_ready"), sem("gates_ready")
        ch_fin = sem("ch_fin")
        h_stored, x2T_stored = sem("h_stored"), sem("x2T_stored")
        wl, up, gelu, down, acc = sem("w_loaded"), sem("up"), sem("gelu_done"), sem("down"), sem("acc")
        ups = sem("ups")
        NH = BT * P // 1024
        ch_moe = sem("ch_moe")
        st = sem("stored")
        v_cur_ready, ch_a2 = sem("v_cur_ready"), sem("ch_a2")

        block = ctx.enter_context(nc.Block())

        N_LN = 7 + 12
        N_PRE = 2
        N_FIN = 17
        N_PC = 7
        N_CONST = 15

        @block.sync
        def _(sp):
            sp.dma_start(xas[:], xa).then_inc(ld, 16)
            sp.dma_start(xbs[:], xb).then_inc(ld, 16)
            sp.dma_start(x0s[:], x0.broadcast_to([P, B * C])).then_inc(ld, 16)
            sp.dma_start(waT[:], attn_w).then_inc(ld, 16)
            sp.dma_start(rwT[:], router_w).then_inc(ld, 16)
            sp.dma_start(rb[:], router_b.broadcast_to([P, E])).then_inc(ld, 16)
            sp.wait_ge(pchain, N_PC)
            sp.dma_start(bias0[0:1, :], tok_b).then_inc(ld, 16)
            srcs = [w4[k * P:(k + 1) * P, :] for k in range(4)] + [w3x, w3y]
            for k, src in enumerate(srcs):
                if k >= 2:
                    sp.wait_ge(w_split, k - 1)
                sp.dma_start(wstage[:, k % 2, :], src).then_inc(ldw[k % 2], 16)

            def store(f):
                sp.wait_ge(x2T_ready, f + 1)
                sp.dma_start(x2T_all[:, bass.ds(f * (T * P), T * P)], x2T[:]).then_inc(x2T_stored, 16)
                sp.dma_start(h_all[:, bass.ds(f * T, T), :], h1[:]).then_inc(h_stored, 16)

            with sp.Fori(0, B) as f:
                store(f)

            sp.wait_ge(x2T_stored, 16 * B)
            with sp.Fori(0, E) as e:
                sp.wait_ge(acc, e * BT)
                sp.dma_start(w1s, w1[bass.ds(e, 1), :, :].rearrange("a p f -> (a p) f")).then_inc(wl, 16)
                sp.dma_start(w2s, w2[bass.ds(e, 1), :, :, :].rearrange("a p c d -> (a p) c d")).then_inc(wl, 16)
                sp.dma_start(b1s[:], b1[bass.ds(e, 1), :, :].rearrange("a p c -> (a p) c")).then_inc(wl, 16)
                sp.dma_start(b2s, b2[bass.ds(e, 1), :].broadcast_to([P, D])).then_inc(wl, 16)
                with sp.Fori(0, NH) as n:
                    for u in range(2):
                        sp.wait_ge(ups, e * NH + n if u == 0 else e * NH + n)
                        sp.dma_start(x2T_blk[:, u, :], x2T_all[:, bass.ds(n * 1024 + u * 512, 512)]).then_inc(xl[u], 16)
            sp.wait_ge(acc, E * BT)
            sp.wait_ge(ch_moe, E * BT * 1)
            h_view = h_all[:].rearrange("p (b t) d -> p b t d", t=T)
            for t in range(T):
                n = P if t < T - 1 else LAST
                sp.dma_start(out[:, t * P:t * P + n, :].rearrange("b p d -> p b d"),
                             h_view[0:n, :, t, :]).then_inc(st, 16)
            sp.wait_ge(st, 16 * T)

        @block.gpsimd
        def _(pool):
            g = nc.gpsimd
            link = Link(pool, pchain, 0, N_PC)
            g.memset(ones[:], 1.0).then_inc(consts, 1)
            link(g.memset(bias0[:], 0.0))
            g.memset(v_all[:, B * T * C:], 0.0).then_inc(consts, 1)
            g.memset(a1_all[:, B * T * C:], 0.0).then_inc(consts, 1)
            g.memset(b1_all[:, B * T * C:], 0.0).then_inc(consts, 1)
            g.memset(d1_all[:, B * T * C:], 0.0).then_inc(consts, 1)
            g.memset(carry[:, 0, :], 0.0).then_inc(consts, 1)
            g.memset(run2[:, 0, :], 0.0).then_inc(consts, 1)
            link(g.memset(pack[:, :, 192:256], 0.0))
            g.memset(pack[:, :, 208:209], 1.0).then_inc(consts, 1)
            g.memset(pack[:, :, 232:233], 1.0).then_inc(consts, 1)
            link(g.memset(ident[:], 0.0))
            g.affine_select(out=ident[:], in_=ident[:], compare_op=ALU.not_equal, fill=1.0, base=0,
                            pattern=[[-1, P]], channel_multiplier=1).then_inc(consts, 1)
            link(g.memset(before[:], 1.0))
            g.affine_select(out=before[:], in_=before[:], compare_op=ALU.is_gt, fill=0.0, base=0,
                            pattern=[[1, P + 1]], channel_multiplier=-1).then_inc(consts, 1)
            link(g.memset(upto[:], 1.0))
            g.affine_select(out=upto[:], in_=upto[:], compare_op=ALU.is_ge, fill=0.0, base=0,
                            pattern=[[1, P]], channel_multiplier=-1).then_inc(consts, 1)
            link(g.memset(ident16[:], 0.0))
            g.affine_select(out=ident16[:], in_=ident16[:], compare_op=ALU.not_equal, fill=1.0, base=0,
                            pattern=[[-1, P]], channel_multiplier=1).then_inc(consts, 1)
            link(g.memset(future[:], MASKED))
            g.affine_select(out=future[:], in_=future[:], compare_op=ALU.is_gt, fill=0.0, base=0,
                            pattern=[[1, P]], channel_multiplier=-1).then_inc(consts, 1)
            g.iota(iotai[:], [[0, T], [1, E]], base=0, channel_multiplier=0).then_inc(consts, 1)
            link.end()
            pool.wait_ge(consts, N_CONST)
            pool.wait_ge(paths, 4)

            def run2_of(b):
                pool.wait_ge(inc2_ready, b + 1)
                after(pool, s2_sum, b)
                link = Link(pool, ch_run2, b * (T - 2), T - 2)
                for i in range(T - 1):
                    ins = g.tensor_tensor(run2[:, i + 1, :], run2[:, i, :], inc2[:, i, :], ALU.add)
                    if i < T - 2:
                        link(ins)
                ins.then_inc(run2_ready, 1)
                link.end()

            def loc3_of(b, i, v):
                pool.wait_ge(a2_ready, b + 1)
                after(pool, a3_sum, 2 * T * b + 2 * i - 2)
                g.tensor_tensor(loc3[:, i % 2, :].rearrange("p (a c) -> p a c", c=C),
                                c2[:, i, :].unsqueeze(2).broadcast_to([P, 64, C]),
                                v[:, i, :].unsqueeze(1).broadcast_to([P, 64, C]),
                                ALU.mult).then_inc(loc3_ready, 1)

            def rundy_of(b, i):
                pool.wait_ge(weighted, 2 * T * b + 2 * i + 2)
                after(pool, path_sum, b * T + i)
                if i >= 1:
                    pool.wait_ge(rundy_ready, (T - 1) * b + i)
                prev = bias0[:] if i == 0 else rundy[:, i % 2, :]
                g.tensor_tensor(rundy[:, (i + 1) % 2, :], prev, dy[:, i % 2, :], ALU.add)\
                    .then_inc(rundy_ready, 1)

            def save_h(a):
                pool.wait_ge(h_ready, T * a + T)
                after(pool, x2_ready, a)
                after(pool, h_stored, a * 16)
                g.tensor_tensor(h1[:], hb[:], carry[:, 0, 0:1].unsqueeze(2).broadcast_to([P, T, D]), ALU.add).then_inc(h_saved, 1)

            def body(b, tok, att):
                if att:
                    save_h(b - 1)
                if tok:
                    pool.wait_ge(v_cur_ready, b + 1)
                    for i in range(T):
                        if i >= 1:
                            rundy_of(b, i - 1)
                        if i + 2 < T:
                            loc3_of(b, i + 2, v_cur)
                        if i == 2:
                            run2_of(b + 1)
                        if i == T - 1:
                            loc3_of(b + 1, 0, v_nxt)
                            loc3_of(b + 1, 1, v_nxt)

            run2_of(0)
            loc3_of(0, 0, v_nxt)
            loc3_of(0, 1, v_nxt)
            body(0, True, False)
            with pool.Fori(1, B) as b:
                body(b, True, True)
            body(B, False, True)

        @block.scalar
        def _(act):
            a_ = nc.scalar
            for k in range(6):
                act.wait_ge(ldw[k % 2], 16 * (k // 2 + 1))
                a_.activation(w4h[:, k, :], wstage[:, k % 2, :], ACT.Copy).then_inc(w_hi, 1)
            act.wait_ge(consts, N_CONST)

            def hi_of(b, i):
                for h in range(2):
                    act.wait_ge(a3_sum, 2 * T * b + 2 * i + h + 1)
                    if h == 0:
                        after(act, main_done, 2 * T * b + 2 * i - 2)
                        if i == 0:
                            pass
                        else:
                            act.wait_ge(a3_lo, 2 * T * b + 2 * i)
                    for k in (2 * h, 2 * h + 1):
                        ins = a_.activation(a3h[:, i % 2, k * P:(k + 1) * P],
                                            psA[:, h, (k % 2) * 129:(k % 2) * 129 + P],
                                            ACT.Identity, bias=carry[:, i, k:k + 1])
                    ins.then_inc(a3_hi, 1)

            def packT_of(b, i):
                act.wait_ge(pack_sum, T * b + i + 1)
                a_.activation(packT[:, i % 2, :], psS[:, 0:256], ACT.Copy).then_inc(pack_copied, 1)

            def h_of(b, i):
                act.wait_ge(path_sum, T * b + i + 1)
                if i == 0:
                    after(act, h_saved, b)
                    after(act, x1_ready, b)
                a_.activation(hb[:, i, :], psS[:, 0:P], ACT.Copy).then_inc(h_ready, 1)

            def x1T_copy(a):
                act.wait_ge(x1T_psum, a + 1)
                a_.activation(x1T[:], psW[:, 0:T * P], ACT.Copy).then_inc(x1T_ready, 1)

            def k_copy(a):
                act.wait_ge(k_psum, a + 1)
                a_.activation(kT[:], psW[:, 0:T * P], ACT.Copy)
                a_.activation(kk[:, 4:6, :], psW[:, T * P:(T + 2) * P], ACT.Copy).then_inc(k_ready, 1)

            def exp_of(a, gi):
                act.wait_ge(negmax_ready, 4 * a + gi + 1)
                for q in GROUPS[gi]:
                    n = (q + 1) * P
                    ins = a_.activation(probs[:, PLACE[q]:PLACE[q] + n], psW[:, PLACE[q]:PLACE[q] + n],
                                        ACT.Exp, bias=negmax[:, q:q + 1], accum_out=rowsum[:, q:q + 1])
                ins.then_inc(exp_ready, 1)

            def pT_copy(a, gi):
                n = max(PLACE[q] + (q + 1) * P for q in GROUPS[gi])
                act.wait_ge(pT_psum, 4 * a + gi + 1)
                a_.activation(probsT[:, 0:n], psW[:, 0:n], ACT.Copy).then_inc(pT_ready, 1)

            def x2T_copy(f):
                act.wait_ge(x2T_psum, f + 1)
                after(act, x2T_stored, 16 * f)
                a_.activation(x2T[:], psW[:, 0:T * P], ACT.Copy).then_inc(x2T_ready, 1)

            def router_exp(f):
                act.wait_ge(lg_ready, f + 1)
                a_.activation(pr[:], lg[:], ACT.Exp).then_inc(pr_ready, 1)

            def body(b, tok, att, fin):
                a, f = b - 1, b - 2
                if att:
                    h_of(a, T - 1)
                for i in range(T):
                    if tok and i + 1 < T:
                        hi_of(b, i + 1)
                        packT_of(b, i + 1)
                    if tok and i >= 1:
                        h_of(b, i - 1)
                    if i == 0 and fin:
                        x2T_copy(f)
                    if i == 1 and fin:
                        router_exp(f)
                    if att:
                        if i == 0:
                            x1T_copy(a)
                        if i == 1:
                            k_copy(a)
                            exp_of(a, 0)
                        if i >= 2:
                            pT_copy(a, i - 2)
                            if i - 1 < 4:
                                exp_of(a, i - 1)
                if tok:
                    hi_of(b + 1, 0)
                    packT_of(b + 1, 0)

            hi_of(0, 0)
            packT_of(0, 0)
            body(0, True, False, False)
            body(1, True, True, False)
            with act.Fori(2, B) as b:
                body(b, True, True, True)
            body(B, False, True, True)
            x2T_copy(B - 1)
            router_exp(B - 1)

            NBLK = BT * P // 512
            with act.Fori(0, E) as e:
                with act.Fori(0, NBLK) as n:
                    act.wait_ge(wl, 64 * e + 64)
                    for c in range(4):
                        act.wait_ge(up, (e * NBLK + n) * 4 + c + 1)
                        a_.activation(hT[c], psP[:, c % 2, :], ACT.Gelu,
                                      bias=b1s[:, c:c + 1]).then_inc(gelu, 1)

        @block.vector
        def _(dve):
            d = nc.vector
            dve.wait_ge(ld, 16 * 7)
            n0 = B * T * C
            link = Link(dve, ch_setup, 0, 4)
            d.tensor_tensor(v_all[:, 0:n0], xbs[:], xas[:], ALU.subtract).then_inc(paths, 1)
            x0b = x0s[:].rearrange("p (b c) -> p b c", c=C).unsqueeze(2).broadcast_to([P, B, T, C])
            link(d.tensor_tensor(xas[:].rearrange("p (b t c) -> p b t c", t=T, c=C),
                                 xas[:].rearrange("p (b t c) -> p b t c", t=T, c=C), x0b, ALU.subtract))
            dve.wait_ge(paths, 1)
            d.scalar_tensor_tensor(a1_all[:, 0:n0], v_all[:, 0:n0], 0.5, xas[:], ALU.mult, ALU.add).then_inc(paths, 1)
            link(d.tensor_scalar(xbs[:], xas[:], 0.5, None, ALU.mult))
            d.scalar_tensor_tensor(b1_all[:, 0:n0], v_all[:, 0:n0], 1.0 / 6, xbs[:], ALU.mult, ALU.add).then_inc(paths, 1)
            link(d.tensor_scalar(xas[:], xas[:], 1.0 / 6, None, ALU.mult))
            d.scalar_tensor_tensor(d1_all[:, 0:n0], v_all[:, 0:n0], 1.0 / 24, xas[:], ALU.mult, ALU.add).then_inc(paths, 1)
            dve.wait_ge(paths, 4)
            dve.wait_ge(consts, N_CONST)
            link(d.tensor_copy(iota16[:], iotai[:]))
            link.end()
            for k in range(6):
                dve.wait_ge(w_hi, k + 1)
                d.tensor_tensor(w4l[:, k, :], wstage[:, k % 2, :], w4h[:, k, :].bitcast(F32),
                                ALU.subtract).then_inc(w_split, 1)
            dve.wait_ge(w_split, 6)
            d.tensor_copy(w4l[64:96, 5, :], w4h[64:96, 5, :].bitcast(F32)).then_inc(w_split, 1)

            def outer(out_, left, right, n, k):
                return d.tensor_tensor(out_, left.unsqueeze(n).broadcast_to(k),
                                       right.unsqueeze(n - 1).broadcast_to(k), ALU.mult)

            def inc2_of(b):
                cols = bass.ds(b * (T * C), T * C)
                flat = v_nxt[:].rearrange("p t c -> p (t c)")
                after(dve, loc3_ready, T * (b - 1) + 2)
                after(dve, s2_sum, b)
                link = Link(dve, ch_pre, b * N_PRE, N_PRE)
                link(d.tensor_scalar(flat, v_all[:, cols], 1.0, None, ALU.mult))
                k4 = [P, T, C, C]
                v4 = v_nxt[:].unsqueeze(2).broadcast_to(k4)
                for src, dst in ((a1_all, inc2), (b1_all, t1), (d1_all, t2)):
                    left = src[:, cols].rearrange("p (t c) -> p t c", c=C).unsqueeze(3).broadcast_to(k4)
                    ins = d.tensor_tensor(dst[:].rearrange("p t (i j) -> p t i j", j=C), left, v4, ALU.mult)
                    if dst is inc2:
                        ins.then_inc(inc2_ready, 1)
                link(ins)
                link.end()

            def a2_of(b):
                s2 = psS[:, 0:T * 64].rearrange("p (t n) -> p t n", n=64)
                dve.wait_ge(s2_sum, b + 1)
                after(dve, loc3_ready, T * b)
                after(dve, pack_sum, T * b)
                link = Link(dve, ch_a2, 3 * b, 3)
                cols = bass.ds(b * (T * C), T * C)
                a1v = a1_all[:, cols].rearrange("p (t c) -> p t c", c=C)
                link(d.tensor_scalar(pack[:, :, 192:200].bitcast(F32R), a1v, 1.0, None, ALU.mult))
                d.tensor_tensor(pack[:, :, 200:208], a1v, pack[:, :, 192:200], ALU.subtract)
                d.tensor_copy(pack[:, :, 224:232], pack[:, :, 192:200])
                d.scalar_tensor_tensor(c2[:], s2, 0.5, t2[:], ALU.mult, ALU.add)
                link(d.tensor_tensor(a2[:], s2, t1[:], ALU.add))
                link(d.tensor_copy(pack[:, :, 0:64].bitcast(F32R), a2[:]))
                d.tensor_tensor(pack[:, :, 64:128], a2[:], pack[:, :, 0:64], ALU.subtract)
                d.tensor_copy(pack[:, :, 128:192], pack[:, :, 0:64]).then_inc(a2_ready, 1)
                link.end()

            def inc3_of(b, i, v):
                after(dve, a3_sum, 2 * T * b + 2 * i - 2)
                d.tensor_tensor(inc3[:, i % 2, :].rearrange("p (a c) -> p a c", c=C),
                                a2[:, i, :].unsqueeze(2).broadcast_to([P, 64, C]),
                                v[:, i, :].unsqueeze(1).broadcast_to([P, 64, C]),
                                ALU.mult).then_inc(inc3_ready, 1)

            def lo_of(b, i):
                for h in range(2):
                    dve.wait_ge(a3_hi, 2 * T * b + 2 * i + h + 1)
                    for k in (2 * h, 2 * h + 1):
                        d.scalar_tensor_tensor(a3l[:, i % 2, k * P:(k + 1) * P],
                                               psA[:, h, (k % 2) * 129:(k % 2) * 129 + P],
                                               carry[:, i, k:k + 1],
                                               a3h[:, i % 2, k * P:(k + 1) * P].bitcast(F32),
                                               ALU.add, ALU.subtract)
                    d.tensor_tensor(carry[:, i + 1, 2 * h:2 * h + 2], psA[:, h, P:P + 130:129],
                                    carry[:, i, 2 * h:2 * h + 2], ALU.add).then_inc(a3_lo, 1)

            def weigh(b, i, h):
                dve.wait_ge(main_done, 2 * T * b + 2 * i + h + 1)
                if h == 0:
                    after(dve, path_sum, T * b + i - 1)
                    if i != 1:
                        after(dve, rundy_ready, (T - 1) * b + max(i - 1, 0))
                acc_ = dy[:, i % 2, :]
                link = Link(dve, ch_w, (2 * T * b + 2 * i + h) * 3, 3)
                for m in range(LH):
                    blk = psP[:, h, m * D:(m + 1) * D]
                    vl = v_cur[:, i, h * LH + m:h * LH + m + 1]
                    if h == 0 and m == 0:
                        ins = d.tensor_scalar(acc_, blk, vl, None, ALU.mult)
                    else:
                        ins = d.scalar_tensor_tensor(acc_, blk, vl, acc_, ALU.mult, ALU.add)
                    if m < LH - 1:
                        link(ins)
                    else:
                        ins.then_inc(weighted, 1)
                if h == 0:
                    dve.wait_ge(weighted, 2 * T * b + 2 * i + 1)
                link.end()

            def norm(link, stats, src, dst, wait=None):
                for i in range(T):
                    ins = d.bn_stats(stats[:, i, :], src[:, i, :])
                link(ins)
                me, m2e, mo, m2o = (stats[:, :, c] for c in (1, 2, 4, 5))
                mean, dif, var, y, t = (nw[:, c, :] for c in range(5))
                yb_ = nw[:, 3, :].bitcast(U32)
                d.tensor_tensor(mean, me, mo, ALU.add)
                d.tensor_tensor(dif, me, mo, ALU.subtract)
                link(d.tensor_tensor(var, m2e, m2o, ALU.add))
                link(d.tensor_tensor(dif, dif, dif, ALU.mult))
                d.tensor_scalar(mean, mean, 0.5, None, ALU.mult)
                link(d.tensor_scalar(var, var, 1.0 / D, EPS, ALU.mult, ALU.add))
                link(d.scalar_tensor_tensor(var, dif, 0.25, var, ALU.mult, ALU.add))
                link(d.tensor_scalar(yb_, var.bitcast(U32), 1, None, ALU.logical_shift_right))
                link(d.tensor_scalar(yb_, yb_, -1.0, MAGIC, ALU.mult, ALU.add))
                for _ in range(3):
                    link(d.tensor_tensor(t, y, y, ALU.mult))
                    link(d.tensor_tensor(t, t, var, ALU.mult))
                    link(d.tensor_scalar(t, t, -0.5, 1.5, ALU.mult, ALU.add))
                    link(d.tensor_tensor(y, y, t, ALU.mult))
                for i in range(T):
                    ins = d.tensor_scalar(dst[:, i, :], src[:, i, :], nw[:, 0, i:i + 1], nw[:, 3, i:i + 1],
                                          ALU.subtract, ALU.mult)
                return ins

            def ln1(a):
                dve.wait_ge(h_ready, T * a + T)
                link = Link(dve, ch_ln1, a * N_LN, N_LN)
                norm(link, st1, hb, x1).then_inc(x1_ready, 1)
                link.end()

            def k_copy(a):
                dve.wait_ge(k_psum, a + 1)
                d.tensor_copy(kk[:, 0:4, :], psO[:].rearrange("p (k e) -> p k e", e=D)).then_inc(k_ready2, 1)

            def negmax_of(a, gi):
                dve.wait_ge(scores, 4 * a + gi + 1)
                for q in GROUPS[gi]:
                    n = (q + 1) * P
                    ins = d.tensor_reduce(negmax[:, q:q + 1], psW[:, PLACE[q]:PLACE[q] + n], AX.X, ALU.max,
                                          negate=True)
                ins.then_inc(negmax_ready, 1)

            def attend(a, gi):
                dve.wait_ge(exp_ready, 4 * a + gi + 1)
                qs = GROUPS[gi]
                link = Link(dve, ch_att, (4 * a + gi) * 2, 2)
                link(d.reciprocal(rinv[:, qs[0]:qs[-1] + 1], rowsum[:, qs[0]:qs[-1] + 1]))
                dve.wait_ge(pv_psum, 4 * a + gi + 1)
                for s, q in enumerate(qs):
                    ins = d.scalar_tensor_tensor(x1[:, q, :], psO[:, s * D:(s + 1) * D], rinv[:, q:q + 1],
                                                 x1[:, q, :], ALU.mult, ALU.add)
                link(ins)
                dve.wait_ge(h_saved, a + 1)
                d.tensor_tensor(h1[:, qs[0]:qs[-1] + 1, :], h1[:, qs[0]:qs[-1] + 1, :],
                                x1[:, qs[0]:qs[-1] + 1, :], ALU.add).then_inc(attended, 1)
                link.end()

            def ln2(a):
                dve.wait_ge(attended, 4 * a + 4)
                link = Link(dve, ch_ln2, a * N_LN, N_LN)
                norm(link, st2, h1, x2).then_inc(x2_ready, 1)
                link.end()

            def router_logits(f):
                dve.wait_ge(logits, f + 1)
                link = Link(dve, ch_fin, f * N_FIN, N_FIN)
                link(d.tensor_tensor(lg[:], psO[:, 0:T * E].rearrange("p (t e) -> p t e", e=E),
                                     rb[:].unsqueeze(1).broadcast_to([P, T, E]), ALU.add))
                link(d.tensor_reduce(r6[:, 0, :], lg[:], AX.X, ALU.max))
                d.tensor_tensor(lg[:], lg[:], r6[:, 0, :].unsqueeze(2).broadcast_to([P, T, E]),
                                ALU.subtract).then_inc(lg_ready, 1)
                return link

            def gates_of(f, link):
                def wide(x):
                    return x.unsqueeze(2).broadcast_to([P, T, E])
                dve.wait_ge(pr_ready, f + 1)
                link(d.tensor_reduce(r6[:, 1, :], pr[:], AX.X, ALU.add))
                link(d.reciprocal(r6[:, 2, :], r6[:, 1, :]))
                link(d.tensor_tensor(pr[:], pr[:], wide(r6[:, 2, :]), ALU.mult))
                left = pr[:]
                for n in range(2):
                    link(d.tensor_reduce(r6[:, 3 + n, :], left, AX.X, ALU.max))
                    link(d.tensor_tensor(sel[:, 0, :, :], left, wide(r6[:, 3 + n, :]), ALU.is_lt))
                    link(d.scalar_tensor_tensor(sel[:, 0, :, :], sel[:, 0, :, :], float(E), iota16[:],
                                                ALU.mult, ALU.add))
                    link(d.tensor_reduce(r6[:, 5, :], sel[:, 0, :, :], AX.X, ALU.min))
                    link(d.tensor_tensor(sel[:, 1 + n, :, :], iota16[:], wide(r6[:, 5, :]), ALU.is_equal))
                    if n == 0:
                        link(d.scalar_tensor_tensor(lg[:], sel[:, 1, :, :], -2.0, pr[:], ALU.mult, ALU.add))
                        left = lg[:]
                link(d.tensor_tensor(sel[:, 1, :, :], sel[:, 1, :, :], sel[:, 2, :, :], ALU.add))
                d.tensor_tensor(gates[:, bass.ds(f * T, T), :], sel[:, 1, :, :], pr[:], ALU.mult)\
                    .then_inc(gates_ready, 1)
                link.end()

            def body(b, tok, att, fin):
                a, f = b - 1, b - 2
                if tok:
                    after(dve, loc3_ready, T * b + 2)
                    after(dve, weighted, 2 * T * b)
                    d.tensor_copy(v_cur[:], v_nxt[:]).then_inc(v_cur_ready, 1)
                    dve.wait_ge(v_cur_ready, b + 1)
                link = None
                for i in range(T):
                    if tok:
                        if i + 1 < T:
                            lo_of(b, i + 1)
                        if i + 2 < T:
                            inc3_of(b, i + 2, v_cur)
                        if i == 2:
                            inc2_of(b + 1)
                        if i == T - 1:
                            a2_of(b + 1)
                            inc3_of(b + 1, 0, v_nxt)
                            inc3_of(b + 1, 1, v_nxt)
                        weigh(b, i, 0)
                    if att and i == 0:
                        ln1(a)
                    if att and i == 1:
                        k_copy(a)
                    if tok:
                        weigh(b, i, 1)
                    if fin and i == 0:
                        link = router_logits(f)
                    if fin and i == 1:
                        gates_of(f, link)
                    if att and i >= 1:
                        if i >= 2:
                            attend(a, i - 2)
                        if i - 1 < 4:
                            negmax_of(a, i - 1)
                if att:
                    ln2(a)
                if tok:
                    lo_of(b + 1, 0)

            inc2_of(0)
            a2_of(0)
            inc3_of(0, 0, v_nxt)
            inc3_of(0, 1, v_nxt)
            lo_of(0, 0)
            body(0, True, False, False)
            body(1, True, True, False)
            with dve.Fori(2, B) as b:
                body(b, True, True, True)
            body(B, False, True, True)
            gates_of(B - 1, router_logits(B - 1))

            dve.wait_ge(gates_ready, B)
            dve.wait_ge(h_stored, 16 * B)
            NBLK = BT * P // 512
            with dve.Fori(0, E) as e:
                with dve.Fori(0, NBLK) as n:
                    dve.wait_ge(wl, 64 * e + 64)
                    for c in range(4):
                        tile = n * 4 + c
                        dve.wait_ge(down, (e * NBLK + n) + 1)
                        d.tensor_tensor(yb, psO[:, c * D:(c + 1) * D], b2s, ALU.add).then_inc(ch_moe, 1)
                        dve.wait_ge(ch_moe, (e * NBLK + n) * 4 + c + 1)
                        hh = h_all[:, bass.ds(tile, 1), :].rearrange("p a d -> p (a d)")
                        d.scalar_tensor_tensor(hh, yb,
                                               gates[:, bass.ds(tile, 1), bass.ds(e, 1)].rearrange("p a c -> p (a c)"),
                                               hh, ALU.mult, ALU.add).then_inc(acc, 1)
                        dve.wait_ge(acc, (e * NBLK + n) * 4 + c + 1)

        @block.tensor
        def _(pe):
            t_ = nc.tensor
            pe.wait_ge(consts, N_CONST)

            def s2_of(b):
                pe.wait_ge(inc2_ready, b + 1)
                pe.wait_ge(run2_ready, b + 1)
                after(pe, h_ready, T * (b - 1) + 4)
                o = psS[:, 0:T * 64]
                t_.matmul(o, before[:, 0:P], inc2[:].rearrange("p t n -> p (t n)"), start=True, stop=False)
                t_.matmul(o, ones[:], run2[:].rearrange("p t n -> p (t n)"), start=False, stop=True)\
                    .then_inc(s2_sum, 1)

            def a3_of(b, i):
                pe.wait_ge(inc3_ready, T * b + i + 1)
                pe.wait_ge(loc3_ready, T * b + i + 1)
                after(pe, a3_lo, 2 * T * b + 2 * i)
                for k in range(4):
                    o = psA[:, k // 2, (k % 2) * 129:(k % 2) * 129 + 129]
                    t_.matmul(o, inc3[:, i % 2, k * P:(k + 1) * P], before[:], start=True, stop=False)
                    ins = t_.matmul(o[:, 0:P], loc3[:, i % 2, k * P:(k + 1) * P], ident[:], is_transpose=True,
                                    start=False, stop=True)
                    if k % 2:
                        ins.then_inc(a3_sum, 1)

            def pack_of(b, i):
                pe.wait_ge(a2_ready, b + 1)
                after(pe, h_ready, T * b + (-1, 0, 0, 1, 2, 3)[i])
                after(pe, pack_copied, T * b + i)
                t_.transpose(psS[:, 0:P], pack[:, i, 0:P], ident[:])
                t_.transpose(psS[:, P:2 * P], pack[:, i, P:2 * P], ident[:]).then_inc(pack_sum, 1)

            def main_of(b, i, h):
                after(pe, weighted, 2 * T * b + 2 * i + h - 1)
                if h == 0:
                    pe.wait_ge(a3_lo, 2 * T * b + 2 * i + 2)
                    pe.wait_ge(pack_copied, T * b + i + 1)
                o = psP[:, h, :]
                cols = slice(h * 512, h * 512 + 512)
                first = True
                for k in range(4):
                    hi, lo = (x[:, i % 2, k * P:(k + 1) * P] for x in (a3h, a3l))
                    for left, right in ((lo, w4h), (hi, w4l), (hi, w4h)):
                        t_.matmul(o, left, right[:, k, cols], start=first, stop=False)
                        first = False
                t_.matmul(o, packT[:, i % 2, P:2 * P], w4l[:, 5, cols], start=False, stop=False)
                t_.matmul(o, packT[:, i % 2, 0:P], w4h[:, 4, cols], start=False, stop=True)\
                    .then_inc(main_done, 1)

            def path_of(b, i):
                pe.wait_ge(weighted, 2 * T * b + 2 * i + 2)
                if i >= 1:
                    pe.wait_ge(rundy_ready, (T - 1) * b + i)
                if i <= 3:
                    pe.wait_ge(pack_copied, T * b + i + 3)
                elif i == 4:
                    pe.wait_ge(a2_ready, b + 2)
                else:
                    pe.wait_ge(pack_copied, T * (b + 1) + 1)
                o = psS[:, 0:P]
                run = bias0[:] if i == 0 else rundy[:, i % 2, :]
                t_.matmul(o, upto[:], dy[:, i % 2, :], start=True, stop=False)
                t_.matmul(o, ones[:], run, start=False, stop=True).then_inc(path_sum, 1)

            def x1T_of(a):
                pe.wait_ge(x1_ready, a + 1)
                for i in range(T):
                    ins = t_.transpose(psW[:, i * P:(i + 1) * P], x1[:, i, :], ident[:])
                ins.then_inc(x1T_psum, 1)

            def k_of(a):
                pe.wait_ge(x1T_ready, a + 1)
                after(pe, lg_ready, a)
                t_.matmul(psW[:, 0:512], waT[:], x1T[:, 0:512], start=True, stop=True)
                t_.matmul(psW[:, 512:768], waT[:], x1T[:, 512:768], start=True, stop=True)
                for i in range(T):
                    o = psO[:, i * D:(i + 1) * D] if i < 4 else psW[:, (i + 2) * D:(i + 3) * D]
                    ins = t_.matmul(o, x1T[:, i * P:(i + 1) * P], waT[:], start=True, stop=True)
                ins.then_inc(k_psum, 1)

            def scores_of(a, gi):
                if gi == 0:
                    pe.wait_ge(k_ready, a + 1)
                    pe.wait_ge(k_ready2, a + 1)
                else:
                    pe.wait_ge(pT_ready, 4 * a + gi)
                for q in GROUPS[gi]:
                    base, n = PLACE[q], q * P
                    left = x1T[:, q * P:(q + 1) * P]
                    for c0 in range(0, n, 512):
                        c1 = min(c0 + 512, n)
                        t_.matmul(psW[:, base + c0:base + c1], left, kT[:, c0:c1], start=True, stop=True)
                    o = psW[:, base + n:base + n + P]
                    t_.matmul(o, left, kT[:, n:n + P], start=True, stop=False)
                    ins = t_.matmul(o, ident16[:], future[:], start=False, stop=True)
                ins.then_inc(scores, 1)

            def pT_of(a, gi):
                pe.wait_ge(exp_ready, 4 * a + gi + 1)
                for q in GROUPS[gi]:
                    for k in range(q + 1):
                        c = PLACE[q] + k * P
                        ins = t_.transpose(psW[:, c:c + P], probs[:, c:c + P], ident[:])
                ins.then_inc(pT_psum, 1)

            def pv_of(a, gi):
                pe.wait_ge(pT_ready, 4 * a + gi + 1)
                if gi == 0:
                    pe.wait_ge(k_ready2, a + 1)
                else:
                    pe.wait_ge(attended, 4 * a + gi)
                for s, q in enumerate(GROUPS[gi]):
                    for k in range(q + 1):
                        c = PLACE[q] + k * P
                        ins = t_.matmul(psO[:, s * D:(s + 1) * D], probsT[:, c:c + P], kk[:, k, :],
                                        start=(k == 0), stop=(k == q))
                ins.then_inc(pv_psum, 1)

            def x2T_of(f):
                pe.wait_ge(x2_ready, f + 1)
                for i in range(T):
                    ins = t_.transpose(psW[:, i * P:(i + 1) * P], x2[:, i, :], ident[:])
                ins.then_inc(x2T_psum, 1)

            def logits_of(f):
                pe.wait_ge(x2T_ready, f + 1)
                pe.wait_ge(attended, 4 * f + 4)
                for i in range(T):
                    ins = t_.matmul(psO[:, i * E:(i + 1) * E], x2T[:, i * P:(i + 1) * P], rwT[:],
                                    start=True, stop=True)
                ins.then_inc(logits, 1)

            def body(b, tok, att, fin):
                a, f = b - 1, b - 2
                if att:
                    path_of(a, T - 1)
                for i in range(T):
                    if tok:
                        if i + 1 < T:
                            a3_of(b, i + 1)
                            pack_of(b, i + 1)
                        else:
                            s2_of(b + 1)
                        main_of(b, i, 0)
                        if i >= 1:
                            path_of(b, i - 1)
                    if fin and i == 0:
                        x2T_of(f)
                    if att:
                        if i == 1:
                            k_of(a)
                        if i >= 2:
                            pT_of(a, i - 2)
                    if tok:
                        main_of(b, i, 1)
                    if fin and i == 0:
                        logits_of(f)
                    if att:
                        if i == 0:
                            x1T_of(a)
                        if i >= 2:
                            pv_of(a, i - 2)
                        if 1 <= i < 5:
                            scores_of(a, i - 1)
                if tok:
                    a3_of(b + 1, 0)
                    pack_of(b + 1, 0)

            pe.wait_ge(ld, 16 * 7)
            s2_of(0)
            a3_of(0, 0)
            pack_of(0, 0)
            pe.wait_ge(w_split, 7)
            body(0, True, False, False)
            body(1, True, True, False)
            with pe.Fori(2, B) as b:
                body(b, True, True, True)
            body(B, False, True, True)
            x2T_of(B - 1)
            logits_of(B - 1)

            pe.wait_ge(x2T_stored, 16 * B)
            pe.wait_ge(gates_ready, B)
            NBLK = BT * P // 512
            with pe.Fori(0, E) as e:
                with pe.Fori(0, NH) as n2:
                    pe.wait_ge(wl, 64 * e + 64)
                    for u in range(2):
                        done = (e * NBLK + n2 * 2 + u) * 4
                        pe.wait_ge(xl[u], 16 * (e * NH + n2 + 1))
                        for c in range(4):
                            if c >= 2:
                                pe.wait_ge(gelu, done + c - 1)
                            ins = t_.matmul(psP[:, c % 2, :], w1s[:, c * P:(c + 1) * P],
                                      x2T_blk[:, u, :], start=True, stop=True).then_inc(up, 1)
                        pe.wait_ge(gelu, done + 4)
                        pe.wait_ge(acc, done)
                        for s in range(4):
                            for c in range(4):
                                ins = t_.matmul(psO[:, s * D:(s + 1) * D], hT[c][:, s * P:(s + 1) * P], w2s[:, c, :],
                                                start=(c == 0), stop=(c == 3))
                        ins.then_inc(down, 1)
                    t_.matmul(psW[:, 0:2], ident[:], ident[:, 0:2], start=True, stop=True).then_inc(ups, 1)


def kernel(x, L0_tok_W, L0_tok_b, L0_attn_W, L0_ffn_router_w, L0_ffn_router_b, L0_ffn_w1, L0_ffn_b1,
           L0_ffn_w2, L0_ffn_b2):
    import numpy as np
    import concourse.bacc as bacc
    from concourse.bass_utils import run_bass_kernel_spmd

    f32 = np.float32
    x = np.asarray(x)
    n = STEPS + 1
    time = np.arange(n, dtype=f32) * f32(1.0 / STEPS)
    time[-1] = 1.0
    path = np.concatenate([np.broadcast_to(time[:, None, None], (n, B, 1)), x.transpose(1, 0, 2)], axis=2)
    path = np.pad(path, ((0, T * P + 1 - n), (0, 0), (0, 0)), mode="edge")

    def tiles(a):
        return np.ascontiguousarray(a.reshape(T, P, B, C).transpose(1, 2, 0, 3).reshape(P, B * T * C))

    W = np.asarray(L0_tok_W)
    W1t, W2t, W3t, W4t = (W[:, lo:lo + C ** k].T.reshape(-1, C * D)
                          for k, lo in ((1, 0), (2, C), (3, C + C ** 2), (4, C + C ** 2 + C ** 3)))
    gap = np.zeros((15, C * D), f32)
    w3y = np.concatenate([W3t, W2t, W2t, W1t, gap, W2t, W1t, np.zeros((23, C * D), f32)])
    w1 = np.asarray(L0_ffn_w1).transpose(0, 2, 1)
    w2 = np.asarray(L0_ffn_w2).transpose(0, 2, 1).reshape(E, FF // P, P, D).transpose(0, 2, 1, 3)
    arrays = {
        "xa": tiles(path[:-1]), "xb": tiles(path[1:]), "x0": path[0].reshape(1, B * C),
        "w4": W4t, "w3x": np.concatenate([W3t, W3t]), "w3y": w3y, "tok_b": np.asarray(L0_tok_b)[None],
        "attn_w": np.asarray(L0_attn_W).T, "router_w": np.asarray(L0_ffn_router_w).T,
        "router_b": np.asarray(L0_ffn_router_b)[None],
        "w1": w1, "b1": np.asarray(L0_ffn_b1).reshape(E, FF // P, P).transpose(0, 2, 1),
        "w2": w2, "b2": np.asarray(L0_ffn_b2),
    }
    arrays = {k: np.ascontiguousarray(a) for k, a in arrays.items()}
    nc = bacc.Bacc("TRN2", target_bir_lowering=False, num_devices=1)
    aps = {k: nc.dram_tensor(k, a.shape, mybir.dt.from_np(a.dtype), kind="ExternalInput").ap()
           for k, a in arrays.items()}
    out = nc.dram_tensor("out", (B, STEPS, D), F32, kind="ExternalOutput").ap()
    build(nc, out=out, **aps)
    return run_bass_kernel_spmd(nc, [arrays], core_ids=[0]).results[0]["out"]
```

```python
from contextlib import ExitStack

import concourse.bass as bass
from concourse import mybir

F32 = mybir.dt.float32
F32R = mybir.dt.float32r
BF16 = mybir.dt.bfloat16
U32 = mybir.dt.uint32
ALU = mybir.AluOpType
ACT = mybir.ActivationFunctionType
AX = mybir.AxisListType

P = 128
B = 16
STEPS = 749
T = 6
LAST = STEPS - (T - 1) * P
C = 8
D = 128
E = 16
FF = 512
LH = 4
EPS = 1e-5
MASKED = -1e30
SLOT = 256
REGION = 12288
SLOTS = 110
SLOTX = SLOTS + 2
RING = 4
ROW = D + 4
DUMMY = E * REGION
SPILL = DUMMY + SLOT
OUT_ROWS = B * STEPS
assert (2 * OUT_ROWS + E * (SLOT - 1)) // SLOT <= SLOTS and OUT_ROWS + SLOT <= REGION
MAGIC = float(0x5F3759DF)
GROUPS = [[0, 1, 2], [3], [4], [5]]
PLACE = {0: 0, 2: P, 1: 4 * P, 3: 0, 4: 0, 5: 0}


def after(eng, sem, value):
    if not isinstance(value, int) or value > 0:
        eng.wait_ge(sem, value)


class Link:

    def __init__(self, eng, sem, base, per):
        self.eng, self.sem, self.base, self.per, self.n = eng, sem, base, per, 0

    def __call__(self, instruction):
        self.n += 1
        instruction.then_inc(self.sem, 1)
        self.eng.wait_ge(self.sem, self.base + self.n)

    def end(self):
        assert self.n == self.per, (self.n, self.per)


def build(nc, xa, xb, x0, w4, w3x, w3y, tok_b, attn_w, router_w, router_b, w1, b1, w2, b2, out):
    ctx = ExitStack()
    with ctx:
        def sb(name, shape, dt=F32):
            return ctx.enter_context(nc.sbuf_tensor(name, shape, dt))

        def sem(name):
            return ctx.enter_context(nc.semaphore(name))

        BT = B * T
        ident = sb("ident", [P, P])
        ones = sb("ones", [P, P])
        before = sb("before", [P, P + 1])
        upto = sb("upto", [P, P])
        last_row = sb("last_row", [P, P])
        ident16 = sb("ident16", [P, P], BF16)
        future = sb("future", [P, P], BF16)
        waT = sb("waT", [P, D])
        rwT = sb("rwT", [P, E])
        rb = sb("rb", [P, E])
        bias0 = sb("bias0", [P, D])
        iota16 = sb("iota16", [P, T, E])
        iotai = sb("iotai", [P, T, E], mybir.dt.int32)
        NB1 = B + 1
        xas = sb("xas", [P, B * T * C])
        xbs = sb("xbs", [P, B * T * C])
        x0s = sb("x0s", [P, B * C])
        v_all = sb("v_all", [P, NB1 * T * C])
        a1_all = sb("a1_all", [P, NB1 * T * C])
        b1_all = sb("b1_all", [P, NB1 * T * C])
        d1_all = sb("d1_all", [P, NB1 * T * C])
        
        v_cur = sb("v_cur", [P, T, C])
        v_nxt = sb("v_nxt", [P, T, C])
        inc2 = sb("inc2", [P, T, 64])
        run2 = sb("run2", [P, T, 64])
        t1 = sb("t1", [P, T, 64])
        t2 = sb("t2", [P, T, 64])
        a2 = sb("a2", [P, T, 64])
        c2 = sb("c2", [P, T, 64])
        pack = sb("pack", [P, T, 256])
        inc3 = sb("inc3", [P, 2, 512])
        loc3 = sb("loc3", [P, 2, 512])
        carry = sb("carry", [P, T + 1, 4])
        a3h = sb("a3h", [P, 2, 512], F32R)
        a3l = sb("a3l", [P, 2, 512], F32R)
        packT = sb("packT", [P, 2, 256], F32R)
        dyp = sb("dyp", [P, 2, D])
        dy = sb("dy", [P, 2, D])
        hb = sb("hb", [P, T, D])
        h1 = sb("h1", [P, T, D])
        x1 = sb("x1", [P, T, D])
        x1T = sb("x1T", [P, T * P])
        kT = sb("kT", [P, T * P])
        kk = sb("kk", [P, T, D])
        negmax = sb("negmax", [P, T])
        rowsum = sb("rowsum", [P, T])
        rinv = sb("rinv", [P, T])
        probs = sb("probs", [P, T * P])
        probsT = sb("probsT", [P, T * P])
        st1 = sb("st1", [P, T, 6])
        st2 = sb("st2", [P, T, 6])
        nw1 = sb("nw1", [P, 6, T])
        nw2 = sb("nw2", [P, 6, T])
        x2 = sb("x2", [P, T, D])
        x2T = sb("x2T", [P, T * P])
        lg = sb("lg", [P, T, E])
        pr = sb("pr", [P, T, E])
        sel = sb("sel", [P, 3, T, E])
        r6 = sb("r6", [P, 7, T])
        valid = sb("valid", [P, 1])
        mask = sb("mask", [P, T, E])
        cnt = sb("cnt", [P, 2, E])
        eoff = sb("eoff", [P, T, E])
        eoffi = sb("eoffi", [P, T, E], mybir.dt.int32)
        tpos = sb("tpos", [P, T, E])
        pos = sb("pos", [P, 2, T])
        posu = sb("posu", [P, 2, T], U32)
        spill = sb("spill", [P, 2])
        spilli = sb("spilli", [P, 2], mybir.dt.int32)
        invalid = sb("invalid", [P, 1])
        dest = sb("dest", [P, T])
        desti = sb("desti", [P, T], mybir.dt.int32)
        xrow = sb("xrow", [P, T, ROW])
        fill = sb("fill", [P, 2, ROW])
        filli = sb("filli", [P, 2], mybir.dt.int32)
        w1_all = sb("w1_all", [P, E, FF])
        b1_all_e = sb("b1_all_e", [P, E, FF // P])
        iotaj = sb("iotaj", [P, SLOTX])
        iotaji = sb("iotaji", [P, SLOTX], mybir.dt.int32)
        tiles_i = sb("tiles_i", [P, 1], mybir.dt.int32)
        tiles_f = sb("tiles_f", [P, 2])
        ind = sb("ind", [P, 2, SLOTX])
        slot_f = sb("slot_f", [P, 3, SLOTX])
        slot_i = sb("slot_i", [P, 2, SLOTX], mybir.dt.int32)
        seen_i = sb("seen_i", [P, RING, SLOTX], mybir.dt.int32)
        fillrow = sb("fillrow", [P, E], mybir.dt.int32)
        xg = sb("xg", [P, 4, 2 * ROW])
        gate = sb("gate", [P, 2, 2])
        gtmp = sb("gtmp", [P, 2, 2, 2])
        destu = sb("destu", [P, RING, 2], U32)
        b1c = sb("b1c", [P, 2, 4])
        yr = sb("yr", [P, RING, 2 * D])
        zero1 = sb("zero1", [P, 2])
        sorted_x = nc.dram_tensor("sorted_x", [SPILL + B * SLOT, ROW], F32).ap()
        first_count = nc.dram_tensor("first_count", [1, RING], F32).ap()
        wstage = [w1_all[:, 2 * k:2 * k + 2, :].rearrange("p e f -> p (e f)") for k in range(6)]
        w1c = [inc3[:, 0, :], inc3[:, 1, :]]
        xTc = [loc3[:, 0, 0:SLOT], loc3[:, 1, 0:SLOT]]
        split_ctx = ExitStack()
        w4h = split_ctx.enter_context(nc.sbuf_tensor("w4h", [P, 6, 1024], F32R))
        w4l = split_ctx.enter_context(nc.sbuf_tensor("w4l", [P, 6, 1024], F32R))
        split_ctx.close()
        w2_all = sb("w2_all", [P, E * (FF // P), D])
        b2_all = sb("b2_all", [P, E * D])
        hTc = sb("hTc", [P, 2, 4, SLOT])

        psP = ctx.enter_context(nc.psum_tensor("psP", [P, 2, 512], F32))
        psA = ctx.enter_context(nc.psum_tensor("psA", [P, 2, 512], F32))
        psS = ctx.enter_context(nc.psum_tensor("psS", [P, 512], F32))
        psO = ctx.enter_context(nc.psum_tensor("psO", [P, 512], F32))
        psW = ctx.enter_context(nc.psum_tensor("psW", [P, 1024], F32))
        psH = [psP[:].rearrange("p a b -> p (a b)"), psA[:].rearrange("p a b -> p (a b)")]
        psX, psY = psS, [psO[:, 0:2 * D], psW[:, 0:2 * D]]

        ld = sem("loaded_small")
        ldw = [sem(f"loaded_w{k}") for k in range(6)]
        w_split = sem("w_split")
        w_hi = sem("w_hi")
        consts = sem("consts")
        pchain = sem("pool_chain")
        paths = sem("paths")
        inc2_ready, run2_ready, s2_sum = sem("inc2_ready"), sem("run2_ready"), sem("s2_sum")
        a2_ready, s2_read = sem("a2_ready"), sem("s2_read")
        inc3_ready, loc3_ready = sem("inc3_ready"), sem("loc3_ready")
        a3_sum, a3_hi, a3_lo = sem("a3_sum"), sem("a3_hi"), sem("a3_lo")
        pack_sum, pack_copied = sem("pack_sum"), sem("pack_copied")
        main_done, weighed, dy_ready = sem("main_done"), sem("weighed"), sem("dy_ready")
        path_sum, h_ready = sem("path_sum"), sem("h_ready")
        ch_pre, ch_run2, ch_setup = sem("ch_pre"), sem("ch_run2"), sem("ch_setup")
        h_saved, x1_ready, x1T_psum, x1T_ready = sem("h_saved"), sem("x1_ready"), sem("x1T_psum"), sem("x1T_ready")
        k_psum, k_ready, k_ready2 = sem("k_psum"), sem("k_ready"), sem("k_ready2")
        scores, negmax_ready, exp_ready = sem("scores"), sem("negmax_ready"), sem("exp_ready")
        pT_psum, pT_ready, pv_psum, attended = sem("pT_psum"), sem("pT_ready"), sem("pv_psum"), sem("attended")
        x1_scale, x1_upper, x2_scale, x2_upper = sem("x1_scale"), sem("x1_upper"), sem("x2_scale"), sem("x2_upper")
        ch_ln1, ch_ln2, ch_att = sem("ch_ln1"), sem("ch_ln2"), sem("ch_att")
        x2_ready, x2T_psum, x2T_ready, logits = sem("x2_ready"), sem("x2T_psum"), sem("x2T_ready"), sem("logits")
        lg_ready, pr_ready, gates_ready = sem("lg_ready"), sem("pr_ready"), sem("gates_ready")
        ch_fin = sem("ch_fin")
        h_stored = sem("h_stored")
        mask_ready, rank_psum, rank_read, pos_ready, xrow_ready, scattered = (
            sem("mask_ready"), sem("rank_psum"), sem("rank_read"), sem("pos_ready"), sem("xrow_ready"), sem("scattered"))
        spill_ready = sem("spill_ready")
        ch_pos = sem("ch_pos")
        counts, tiles_ready, tiles_sum, ind_ready, slot_sum, table = (
            sem("counts"), sem("tiles_ready"), sem("tiles_sum"), sem("ind_ready"), sem("slot_sum"), sem("table"))
        ch_tab = sem("ch_tab")
        filled = sem("filled")
        wl, wl2 = sem("w1_loaded"), sem("w2_loaded")
        xg_in = [sem(f"xg_in{k}") for k in range(4)]
        xT_psum, xT_ready, w1_ready, up, gelu, down = (
            sem("xT_psum"), sem("xT_ready"), sem("w1_ready"), sem("up"), sem("gelu_done"), sem("down"))
        meta_ready, y_ready, y_seen = sem("meta_ready"), sem("y_ready"), sem("y_seen")
        added = [sem(f"added{k}") for k in range(RING)]
        ch_y, ch_meta = sem("ch_y"), sem("ch_meta")
        st = sem("stored")
        rows_seen = sem("rows_seen")
        st1_done, st2_done = sem("st1_done"), sem("st2_done")
        v_cur_ready, ch_a2 = sem("v_cur_ready"), sem("ch_a2")

        block = ctx.enter_context(nc.Block())

        N_LN = 7 + 9
        N_PRE = 2
        N_FIN = 17
        N_POS = 9
        N_PC = 10
        N_CONST = 24 + 1

        @block.sync
        def _(sp):
            sp.dma_start(xas[:], xa).then_inc(ld, 16)
            sp.dma_start(xbs[:], xb).then_inc(ld, 16)
            sp.dma_start(x0s[:], x0.broadcast_to([P, B * C])).then_inc(ld, 16)
            sp.dma_start(waT[:], attn_w).then_inc(ld, 16)
            sp.dma_start(rwT[:], router_w).then_inc(ld, 16)
            sp.dma_start(rb[:], router_b.broadcast_to([P, E])).then_inc(ld, 16)
            sp.dma_start(b1_all_e[:], b1.rearrange("e p c -> p e c")).then_inc(wl, 16)
            sp.wait_ge(pchain, N_PC)
            sp.dma_start(bias0[0:1, :], tok_b).then_inc(ld, 16)
            srcs = [w4[k * P:(k + 1) * P, :] for k in range(4)] + [w3x, w3y]
            for k, src in enumerate(srcs):
                sp.dma_start(wstage[k], src).then_inc(ldw[k], 16)

            sp.wait_ge(w_split, 6)
            sp.dma_start(w1_all[:], w1.rearrange("e p f -> p e f")).then_inc(wl, 16)
            sp.wait_ge(consts, N_CONST)
            sp.dma_start(out[OUT_ROWS:, :], fill[:, :, 0:D]).then_inc(st, 16)
            sp.dma_start(sorted_x[DUMMY:DUMMY + SLOT, :].rearrange("(p s) c -> p s c", s=2), fill[:]).then_inc(st, 16)

            def store(f):
                sp.wait_ge(attended, 4 * (f + 1))
                n = (T - 1) * P
                sp.dma_start(out[bass.ds(f * STEPS, n), :].rearrange("(t p) d -> p t d", p=P),
                             h1[:, 0:T - 1, :]).then_inc(h_stored, 16)
                sp.dma_start(out[bass.ds(f * STEPS + n, LAST), :], h1[0:LAST, T - 1, :]).then_inc(h_stored, 16)

            with sp.Fori(0, B) as f:
                store(f)

            sp.wait_ge(main_done, 2 * T * B)
            sp.wait_ge(w_split, 7)
            sp.dma_start(w2_all[:].rearrange("p (e c) d -> p e (c d)", e=E), w2.rearrange("e p c d -> p e (c d)")).then_inc(wl2, 16)
            sp.dma_start(b2_all[:], b2.rearrange("(a e) d -> a (e d)", a=1).broadcast_to([P, E * D])).then_inc(wl2, 16)

            sp.wait_ge(table, 1)
            for e in range(0, E, 2):
                r = sp.value_load(fillrow[0:1, e:e + 1], min_val=0, max_val=DUMMY - SLOT)
                sp.dma_start(sorted_x[bass.ds(r, SLOT), :].rearrange("(p s) c -> p s c", s=2), fill[:])\
                    .then_inc(filled, 16)
            sp.wait_ge(filled, 16 * E)
            sp.wait_ge(scattered, 16 * 2 * T * B)
            sp.wait_ge(st, 32)
            sp.wait_ge(h_stored, 32 * B)

            def load_slot(j, k):
                after(sp, xT_psum, j - 3)
                after(sp, meta_ready, j - 3)
                r = sp.value_load(slot_i[0:1, 1, bass.ds(j, 1)] if not isinstance(j, int) else slot_i[0:1, 1, j:j + 1],
                                  min_val=0, max_val=DUMMY)
                sp.dma_start(xg[:, k, :], sorted_x[bass.ds(r, SLOT), :].rearrange("(p s) c -> p (s c)", s=2))\
                    .then_inc(xg_in[k], 16)

            for j in range(4):
                load_slot(j, j)
            with sp.Fori(1, (SLOTS + 2) // 4) as n:
                for k in range(4):
                    load_slot(n * 4 + k, k)
            for k in range(4):
                sp.wait_ge(xg_in[k], 16 * ((SLOTS + 2) // 4))
            for k in range(RING):
                sp.wait_ge(added[k], 16 + 32 * len(range(k, SLOTS, RING)))

        @block.gpsimd
        def _(pool):
            g = nc.gpsimd
            link = Link(pool, pchain, 0, N_PC)
            g.memset(ones[:], 1.0).then_inc(consts, 1)
            link(g.memset(bias0[:], 0.0))
            g.memset(v_all[:, B * T * C:], 0.0).then_inc(consts, 1)
            g.memset(a1_all[:, B * T * C:], 0.0).then_inc(consts, 1)
            g.memset(b1_all[:, B * T * C:], 0.0).then_inc(consts, 1)
            g.memset(d1_all[:, B * T * C:], 0.0).then_inc(consts, 1)
            g.memset(carry[:, 0, :], 0.0).then_inc(consts, 1)
            g.memset(run2[:, 0, :], 0.0).then_inc(consts, 1)
            link(g.memset(pack[:, :, 192:256], 0.0))
            g.memset(pack[:, :, 208:209], 1.0).then_inc(consts, 1)
            g.memset(pack[:, :, 232:233], 1.0).then_inc(consts, 1)
            link(g.memset(ident[:], 0.0))
            g.affine_select(out=ident[:], in_=ident[:], compare_op=ALU.not_equal, fill=1.0, base=0,
                            pattern=[[-1, P]], channel_multiplier=1).then_inc(consts, 1)
            link(g.memset(before[:], 1.0))
            g.affine_select(out=before[:], in_=before[:], compare_op=ALU.is_gt, fill=0.0, base=0,
                            pattern=[[1, P + 1]], channel_multiplier=-1).then_inc(consts, 1)
            link(g.memset(upto[:], 1.0))
            g.affine_select(out=upto[:], in_=upto[:], compare_op=ALU.is_ge, fill=0.0, base=0,
                            pattern=[[1, P]], channel_multiplier=-1).then_inc(consts, 1)
            link(g.memset(last_row[:], 1.0))
            g.affine_select(out=last_row[:], in_=last_row[:], compare_op=ALU.is_ge, fill=0.0, base=1 - P,
                            pattern=[[0, P]], channel_multiplier=1).then_inc(consts, 1)
            link(g.memset(ident16[:], 0.0))
            g.affine_select(out=ident16[:], in_=ident16[:], compare_op=ALU.not_equal, fill=1.0, base=0,
                            pattern=[[-1, P]], channel_multiplier=1).then_inc(consts, 1)
            link(g.memset(fill[:], 0.0))
            g.memset(zero1[:, 0:2], 0.0).then_inc(consts, 1)
            g.memset(cnt[:, 0, :], 0.0).then_inc(consts, 1)
            link(g.memset(valid[:], 1.0))
            g.affine_select(out=valid[:], in_=valid[:], compare_op=ALU.is_gt, fill=0.0, base=LAST,
                            pattern=[[1, 1]], channel_multiplier=-1).then_inc(consts, 1)
            g.iota(eoffi[:], [[0, T], [REGION, E]], base=0, channel_multiplier=0).then_inc(consts, 1)
            g.iota(spilli[:], [[P, 2]], base=SPILL, channel_multiplier=1).then_inc(consts, 1)
            g.iota(desti[:], [[P, T]], base=0, channel_multiplier=1).then_inc(consts, 1)
            g.iota(filli[:], [[1, 2]], base=OUT_ROWS, channel_multiplier=2).then_inc(consts, 1)
            g.iota(iotaji[:], [[1, SLOTX]], base=0, channel_multiplier=0).then_inc(consts, 1)
            link(g.memset(future[:], MASKED))
            g.affine_select(out=future[:], in_=future[:], compare_op=ALU.is_gt, fill=0.0, base=0,
                            pattern=[[1, P]], channel_multiplier=-1).then_inc(consts, 1)
            g.iota(iotai[:], [[0, T], [1, E]], base=0, channel_multiplier=0).then_inc(consts, 1)
            link.end()
            pool.wait_ge(consts, N_CONST - 1)
            g.tensor_copy(fill[:, :, D + 3], filli[:]).then_inc(consts, 1)
            pool.wait_ge(consts, N_CONST)
            for k in range(RING):
                g.dma_start(first_count[:, k:k + 1], zero1[0:1, 0:1]).then_inc(added[k], 16)
            pool.wait_ge(paths, 4)

            def run2_of(b):
                pool.wait_ge(inc2_ready, b + 1)
                after(pool, s2_sum, b)
                link = Link(pool, ch_run2, b * (T - 2), T - 2)
                for i in range(T - 1):
                    ins = g.tensor_tensor(run2[:, i + 1, :], run2[:, i, :], inc2[:, i, :], ALU.add)
                    if i < T - 2:
                        link(ins)
                ins.then_inc(run2_ready, 1)
                link.end()

            def loc3_of(b, i, v):
                pool.wait_ge(a2_ready, b + 1)
                after(pool, a3_sum, 2 * T * b + 2 * i - 2)
                g.tensor_tensor(loc3[:, i % 2, :].rearrange("p (a c) -> p a c", c=C),
                                c2[:, i, :].unsqueeze(2).broadcast_to([P, 64, C]),
                                v[:, i, :].unsqueeze(1).broadcast_to([P, 64, C]),
                                ALU.mult).then_inc(loc3_ready, 1)

            def save_h(a):
                pool.wait_ge(h_ready, T * a + T)
                after(pool, x2_ready, a)
                after(pool, x2_upper, a)
                after(pool, h_stored, a * 32)
                g.tensor_tensor(h1[:], hb[:], carry[:, 0, 0:1].unsqueeze(2).broadcast_to([P, T, D]), ALU.add).then_inc(h_saved, 1)

            def scatter(f, i):
                for k in range(2):
                    g.indirect_dma_start(out=sorted_x, out_offset=bass.IndirectOffsetOnAxis(ap=posu[:, k, i:i + 1], axis=0),
                                         in_=xrow[:, i, :], in_offset=None).then_inc(scattered, 16)

            def rows_ready(f):
                pool.wait_ge(pos_ready, f + 1)
                pool.wait_ge(xrow_ready, f + 1)
                after(pool, rows_seen, f)
                g.tensor_tensor(zero1[:, 1:2], zero1[:, 0:1], zero1[:, 0:1], ALU.add).then_inc(rows_seen, 1)

            def body(b, tok, att, fin):
                if att:
                    save_h(b - 1)
                if tok:
                    pool.wait_ge(v_cur_ready, b + 1)
                for i in range(T):
                    if tok:
                        if i + 2 < T:
                            loc3_of(b, i + 2, v_cur)
                        if i == 2:
                            run2_of(b + 1)
                        if i == T - 1:
                            loc3_of(b + 1, 0, v_nxt)
                            loc3_of(b + 1, 1, v_nxt)
                    if fin and i == 3:
                        rows_ready(b - 2)
                    if fin and i >= 3:
                        scatter(b - 2, 2 * (i - 3))
                        scatter(b - 2, 2 * (i - 3) + 1)

            run2_of(0)
            loc3_of(0, 0, v_nxt)
            loc3_of(0, 1, v_nxt)
            body(0, True, False, False)
            body(1, True, True, False)
            with pool.Fori(2, B) as b:
                body(b, True, True, True)
            body(B, False, True, True)
            body(B + 1, False, False, True)

            def add_slot(j, k):
                cols = slice(j, j + 1) if isinstance(j, int) else bass.ds(j, 1)
                landed = [pool.value_load(seen_i[0:1, m, cols], min_val=16, max_val=16 + 32 * (SLOTS // RING + 1))
                          for m in range(RING)]
                pool.wait_ge(y_ready, j + 1)
                for m in range(RING):
                    pool.wait_ge(added[m], landed[m])
                after(pool, y_seen, j)
                g.tensor_tensor(zero1[:, 1:2], zero1[:, 0:1], zero1[:, 0:1], ALU.add).then_inc(y_seen, 1)
                for s in range(2):
                    g.indirect_dma_start(out=out, out_offset=bass.IndirectOffsetOnAxis(ap=destu[:, k, s:s + 1], axis=0),
                                         in_=yr[:, k, s * D:(s + 1) * D], in_offset=None,
                                         compute_op=ALU.add).then_inc(added[k], 16)

            pool.wait_ge(rows_seen, B)
            pool.wait_ge(table, 1)
            for j in range(SLOTS % RING):
                add_slot(j, j)
            with pool.Fori(0, SLOTS // RING) as n:
                for k in range(RING):
                    add_slot(n * RING + SLOTS % RING + k, (k + SLOTS) % RING)

        @block.scalar
        def _(act):
            a_ = nc.scalar
            act.wait_ge(consts, N_CONST)

            def hi_of(b, i):
                for h in range(2):
                    act.wait_ge(a3_sum, 2 * T * b + 2 * i + h + 1)
                    if h == 0:
                        after(act, main_done, 2 * T * b + 2 * i - 2)
                        if i > 0:
                            act.wait_ge(a3_lo, 2 * T * b + 2 * i)
                    for k in (2 * h, 2 * h + 1):
                        ins = a_.activation(a3h[:, i % 2, k * P:(k + 1) * P],
                                            psA[:, h, (k % 2) * 129:(k % 2) * 129 + P],
                                            ACT.Identity, bias=carry[:, i, k:k + 1])
                    ins.then_inc(a3_hi, 1)

            def packT_of(b, i):
                act.wait_ge(pack_sum, T * b + i + 1)
                a_.activation(packT[:, i % 2, :], psS[:, 0:256], ACT.Copy).then_inc(pack_copied, 1)

            def h_of(b, i):
                act.wait_ge(path_sum, T * b + i + 1)
                if i == 0:
                    after(act, h_saved, b)
                    after(act, x1_ready, b)
                    after(act, x1_upper, b)
                a_.activation(hb[:, i, :], psS[:, 0:P], ACT.Copy).then_inc(h_ready, 1)

            def upper_of(n, scaled, src, dst, nw, done):
                act.wait_ge(scaled, n + 1)
                for i in range(T // 2, T):
                    ins = a_.activation(dst[:, i, :], src[:, i, :], ACT.Identity, bias=nw[:, 5, i:i + 1],
                                        scale=nw[:, 3, i:i + 1])
                ins.then_inc(done, 1)

            def x1T_copy(a):
                act.wait_ge(x1T_psum, a + 1)
                a_.activation(x1T[:], psW[:, 0:T * P], ACT.Copy).then_inc(x1T_ready, 1)

            def k_copy(a):
                act.wait_ge(k_psum, a + 1)
                a_.activation(kT[:], psW[:, 0:T * P], ACT.Copy)
                a_.activation(kk[:, 4:6, :], psW[:, T * P:(T + 2) * P], ACT.Copy).then_inc(k_ready, 1)

            def exp_of(a, gi):
                act.wait_ge(negmax_ready, 4 * a + gi + 1)
                for q in GROUPS[gi]:
                    n = (q + 1) * P
                    ins = a_.activation(probs[:, PLACE[q]:PLACE[q] + n], psW[:, PLACE[q]:PLACE[q] + n],
                                        ACT.Exp, bias=negmax[:, q:q + 1], accum_out=rowsum[:, q:q + 1])
                ins.then_inc(exp_ready, 1)

            def pT_copy(a, gi):
                n = max(PLACE[q] + (q + 1) * P for q in GROUPS[gi])
                act.wait_ge(pT_psum, 4 * a + gi + 1)
                a_.activation(probsT[:, 0:n], psW[:, 0:n], ACT.Copy).then_inc(pT_ready, 1)

            def x2T_copy(f):
                act.wait_ge(x2T_psum, f + 1)
                a_.activation(x2T[:], psW[:, 0:T * P], ACT.Copy).then_inc(x2T_ready, 1)
                after(act, scattered, 16 * 2 * T * f)
                act.wait_ge(x2_ready, f + 1)
                act.wait_ge(x2_upper, f + 1)
                a_.activation(xrow[:, :, 0:D], x2[:], ACT.Copy).then_inc(xrow_ready, 1)

            def router_exp(f):
                act.wait_ge(lg_ready, f + 1)
                a_.activation(pr[:], lg[:], ACT.Exp).then_inc(pr_ready, 1)

            def body(b, tok, att, fin):
                a, f = b - 1, b - 2
                if att:
                    h_of(a, T - 1)
                for i in range(T):
                    if tok and i + 1 < T:
                        packT_of(b, i + 1)
                        hi_of(b, i + 1)
                    if i == 1 and fin:
                        router_exp(f)
                    if tok and i >= 1:
                        h_of(b, i - 1)
                    if i == 0 and fin:
                        upper_of(f, x2_scale, h1, x2, nw2, x2_upper)
                        x2T_copy(f)
                    if att:
                        if i == 0:
                            upper_of(a, x1_scale, hb, x1, nw1, x1_upper)
                            x1T_copy(a)
                        if i == 1:
                            k_copy(a)
                            exp_of(a, 0)
                        if i >= 2:
                            pT_copy(a, i - 2)
                            if i - 1 < 4:
                                exp_of(a, i - 1)
                if tok:
                    packT_of(b + 1, 0)
                    hi_of(b + 1, 0)

            for k in range(6):
                act.wait_ge(ldw[k], 16)
                a_.activation(w4h[:, k, :], wstage[k], ACT.Copy).then_inc(w_hi, 1)
            packT_of(0, 0)
            hi_of(0, 0)
            body(0, True, False, False)
            body(1, True, True, False)
            with act.Fori(2, B) as b:
                body(b, True, True, True)
            body(B, False, True, True)
            upper_of(B - 1, x2_scale, h1, x2, nw2, x2_upper)
            x2T_copy(B - 1)
            router_exp(B - 1)

            act.wait_ge(table, 1)
            for e in range(1, E, 2):
                r = act.value_load(fillrow[0:1, e:e + 1], min_val=0, max_val=DUMMY - SLOT)
                act.dma_start(sorted_x[bass.ds(r, SLOT), :].rearrange("(p s) c -> p s c", s=2), fill[:])\
                    .then_inc(filled, 16)

            def xT_copy(j, u):
                act.wait_ge(xT_psum, j + 1)
                a_.activation(xTc[u], psX[:, 0:SLOT], ACT.Copy).then_inc(xT_ready, 1)

            def gelu_of(j, u):
                act.wait_ge(w1_ready, j + 1)
                for c in range(4):
                    if c % 2 == 0:
                        act.wait_ge(up, 2 * j + c // 2 + 1)
                    ins = a_.activation(hTc[:, u, c, :], psH[u][:, c * SLOT:(c + 1) * SLOT], ACT.Gelu,
                                        bias=b1c[:, u, c:c + 1])
                ins.then_inc(gelu, 1)

            xT_copy(0, 0)
            for j in range(2):
                xT_copy(j + 1, (j + 1) % 2)
                gelu_of(j, j)
            with act.Fori(1, SLOTS // 2) as n:
                for u in range(2):
                    j = n * 2 + u
                    xT_copy(j + 1, 1 - u)
                    gelu_of(j, u)

        @block.vector
        def _(dve):
            d = nc.vector
            dve.wait_ge(ld, 16 * 7)
            n0 = B * T * C
            link = Link(dve, ch_setup, 0, 8)
            d.tensor_tensor(v_all[:, 0:n0], xbs[:], xas[:], ALU.subtract).then_inc(paths, 1)
            x0b = x0s[:].rearrange("p (b c) -> p b c", c=C).unsqueeze(2).broadcast_to([P, B, T, C])
            link(d.tensor_tensor(xas[:].rearrange("p (b t c) -> p b t c", t=T, c=C),
                                 xas[:].rearrange("p (b t c) -> p b t c", t=T, c=C), x0b, ALU.subtract))
            dve.wait_ge(paths, 1)
            d.scalar_tensor_tensor(a1_all[:, 0:n0], v_all[:, 0:n0], 0.5, xas[:], ALU.mult, ALU.add).then_inc(paths, 1)
            link(d.tensor_scalar(xbs[:], xas[:], 0.5, None, ALU.mult))
            d.scalar_tensor_tensor(b1_all[:, 0:n0], v_all[:, 0:n0], 1.0 / 6, xbs[:], ALU.mult, ALU.add).then_inc(paths, 1)
            link(d.tensor_scalar(xas[:], xas[:], 1.0 / 6, None, ALU.mult))
            d.scalar_tensor_tensor(d1_all[:, 0:n0], v_all[:, 0:n0], 1.0 / 24, xas[:], ALU.mult, ALU.add).then_inc(paths, 1)
            dve.wait_ge(paths, 4)
            dve.wait_ge(consts, N_CONST)
            link(d.tensor_copy(iota16[:], iotai[:]))
            d.tensor_copy(eoff[:], eoffi[:])
            d.tensor_copy(dest[:], desti[:])
            d.tensor_copy(iotaj[:], iotaji[:])
            link(d.tensor_copy(spill[:], spilli[:]))
            link(d.tensor_scalar(invalid[:], valid[:], -1.0, 1.0, ALU.mult, ALU.add))
            link(d.tensor_scalar(spill[:], spill[:], invalid[:], None, ALU.mult))
            link(d.tensor_scalar(invalid[:], invalid[:], float(SLOT), None, ALU.mult))
            link.end()
            def outer(out_, left, right, n, k):
                return d.tensor_tensor(out_, left.unsqueeze(n).broadcast_to(k),
                                       right.unsqueeze(n - 1).broadcast_to(k), ALU.mult)

            def inc2_of(b):
                cols = bass.ds(b * (T * C), T * C)
                flat = v_nxt[:].rearrange("p t c -> p (t c)")
                after(dve, loc3_ready, T * (b - 1) + 2)
                after(dve, s2_sum, b)
                link = Link(dve, ch_pre, b * N_PRE, N_PRE)
                link(d.tensor_scalar(flat, v_all[:, cols], 1.0, None, ALU.mult))
                k4 = [P, T, C, C]
                v4 = v_nxt[:].unsqueeze(2).broadcast_to(k4)
                for src, dst in ((a1_all, inc2), (b1_all, t1), (d1_all, t2)):
                    left = src[:, cols].rearrange("p (t c) -> p t c", c=C).unsqueeze(3).broadcast_to(k4)
                    ins = d.tensor_tensor(dst[:].rearrange("p t (i j) -> p t i j", j=C), left, v4, ALU.mult)
                    if dst is inc2:
                        ins.then_inc(inc2_ready, 1)
                link(ins)
                link.end()

            def a2_of(b):
                s2 = psS[:, 0:T * 64].rearrange("p (t n) -> p t n", n=64)
                dve.wait_ge(s2_sum, b + 1)
                after(dve, loc3_ready, T * b)
                after(dve, pack_sum, T * b)
                link = Link(dve, ch_a2, 2 * b, 2)
                d.scalar_tensor_tensor(c2[:], s2, 0.5, t2[:], ALU.mult, ALU.add)
                d.tensor_tensor(a2[:], s2, t1[:], ALU.add).then_inc(s2_read, 1)
                cols = bass.ds(b * (T * C), T * C)
                a1v = a1_all[:, cols].rearrange("p (t c) -> p t c", c=C)
                link(d.tensor_scalar(pack[:, :, 192:200].bitcast(F32R), a1v, 1.0, None, ALU.mult))
                d.tensor_tensor(pack[:, :, 200:208], a1v, pack[:, :, 192:200], ALU.subtract)
                d.tensor_copy(pack[:, :, 224:232], pack[:, :, 192:200])
                dve.wait_ge(s2_read, b + 1)
                link(d.tensor_copy(pack[:, :, 0:64].bitcast(F32R), a2[:]))
                d.tensor_tensor(pack[:, :, 64:128], a2[:], pack[:, :, 0:64], ALU.subtract)
                d.tensor_copy(pack[:, :, 128:192], pack[:, :, 0:64]).then_inc(a2_ready, 1)
                link.end()

            def inc3_of(b, i, v):
                after(dve, a3_sum, 2 * T * b + 2 * i - 2)
                d.tensor_tensor(inc3[:, i % 2, :].rearrange("p (a c) -> p a c", c=C),
                                a2[:, i, :].unsqueeze(2).broadcast_to([P, 64, C]),
                                v[:, i, :].unsqueeze(1).broadcast_to([P, 64, C]),
                                ALU.mult).then_inc(inc3_ready, 1)

            def lo_of(b, i):
                for h in range(2):
                    dve.wait_ge(a3_hi, 2 * T * b + 2 * i + h + 1)
                    for k in (2 * h, 2 * h + 1):
                        d.scalar_tensor_tensor(a3l[:, i % 2, k * P:(k + 1) * P],
                                               psA[:, h, (k % 2) * 129:(k % 2) * 129 + P],
                                               carry[:, i, k:k + 1],
                                               a3h[:, i % 2, k * P:(k + 1) * P].bitcast(F32),
                                               ALU.add, ALU.subtract)
                    d.tensor_tensor(carry[:, i + 1, 2 * h:2 * h + 2], psA[:, h, P:P + 130:129],
                                    carry[:, i, 2 * h:2 * h + 2], ALU.add).then_inc(a3_lo, 1)

            def weigh(b, i, h):
                dve.wait_ge(main_done, 2 * T * b + 2 * i + h + 1)
                n0 = 2 * LH * (T * b + i)
                for m in range(LH):
                    n, blk = h * LH + m, psP[:, h, m * D:(m + 1) * D]
                    vl, part = v_cur[:, i, n:n + 1], dyp[:, m % 2, :]
                    if n == 0:
                        after(dve, dy_ready, T * b + i)
                    if n < 2:
                        ins = d.tensor_scalar(part, blk, vl, None, ALU.mult)
                    else:
                        dve.wait_ge(weighed, n0 + n - 1)
                        ins = d.scalar_tensor_tensor(part, blk, vl, part, ALU.mult, ALU.add)
                    ins.then_inc(weighed, 1)
                if h == 1:
                    after(dve, path_sum, T * b + i - 1)
                    dve.wait_ge(weighed, n0 + 2 * LH)
                    d.tensor_tensor(dy[:, i % 2, :], dyp[:, 0, :], dyp[:, 1, :], ALU.add).then_inc(dy_ready, 1)

            def norm(link, stats, src, dst, rest, nw, scaled):
                for i in rest:
                    ins = d.bn_stats(stats[:, i, :], src[:, i, :])
                link(ins)
                me, m2e, mo, m2o = (stats[:, :, c] for c in (1, 2, 4, 5))
                mean, dif, var, y, t = (nw[:, c, :] for c in range(5))
                yb_ = nw[:, 3, :].bitcast(U32)
                d.tensor_tensor(mean, me, mo, ALU.add)
                d.tensor_tensor(dif, me, mo, ALU.subtract)
                link(d.tensor_tensor(var, m2e, m2o, ALU.add))
                link(d.tensor_tensor(dif, dif, dif, ALU.mult))
                d.tensor_scalar(mean, mean, 0.5, None, ALU.mult)
                link(d.tensor_scalar(var, var, 1.0 / D, EPS, ALU.mult, ALU.add))
                link(d.scalar_tensor_tensor(var, dif, 0.25, var, ALU.mult, ALU.add))
                link(d.tensor_scalar(yb_, var.bitcast(U32), 1, None, ALU.logical_shift_right))
                link(d.tensor_scalar(yb_, yb_, -1.0, MAGIC, ALU.mult, ALU.add))
                for _ in range(3):
                    link(d.scalar_tensor_tensor(t, y, -0.5, y, ALU.mult, ALU.mult))
                    link(d.tensor_tensor(t, t, var, ALU.mult))
                    link(d.scalar_tensor_tensor(y, t, 1.5, y, ALU.add, ALU.mult))
                d.scalar_tensor_tensor(nw[:, 5, :], mean, -1.0, y, ALU.mult, ALU.mult).then_inc(scaled, 1)
                for i in range(T // 2):
                    ins = d.tensor_scalar(dst[:, i, :], src[:, i, :], nw[:, 0, i:i + 1], nw[:, 3, i:i + 1],
                                          ALU.subtract, ALU.mult)
                return ins

            def ln1(a):
                dve.wait_ge(h_ready, T * a + T)
                dve.wait_ge(st1_done, (T - 2) * (a + 1))
                after(dve, x1_upper, a)
                link = Link(dve, ch_ln1, a * N_LN, N_LN)
                norm(link, st1, hb, x1, [T - 2, T - 1], nw1, x1_scale).then_inc(x1_ready, 1)
                link.end()

            def k_copy(a):
                dve.wait_ge(k_psum, a + 1)
                d.tensor_copy(kk[:, 0:4, :], psO[:].rearrange("p (k e) -> p k e", e=D)).then_inc(k_ready2, 1)

            def negmax_of(a, gi):
                dve.wait_ge(scores, 4 * a + gi + 1)
                for q in GROUPS[gi]:
                    n = (q + 1) * P
                    ins = d.tensor_reduce(negmax[:, q:q + 1], psW[:, PLACE[q]:PLACE[q] + n], AX.X, ALU.max,
                                          negate=True)
                ins.then_inc(negmax_ready, 1)

            def attend(a, gi):
                dve.wait_ge(exp_ready, 4 * a + gi + 1)
                qs = GROUPS[gi]
                link = Link(dve, ch_att, (4 * a + gi) * 2, 2)
                link(d.reciprocal(rinv[:, qs[0]:qs[-1] + 1], rowsum[:, qs[0]:qs[-1] + 1]))
                dve.wait_ge(pv_psum, 4 * a + gi + 1)
                for s, q in enumerate(qs):
                    ins = d.scalar_tensor_tensor(x1[:, q, :], psO[:, s * D:(s + 1) * D], rinv[:, q:q + 1],
                                                 x1[:, q, :], ALU.mult, ALU.add)
                link(ins)
                dve.wait_ge(h_saved, a + 1)
                d.tensor_tensor(h1[:, qs[0]:qs[-1] + 1, :], h1[:, qs[0]:qs[-1] + 1, :],
                                x1[:, qs[0]:qs[-1] + 1, :], ALU.add).then_inc(attended, 1)
                link.end()
                if gi < 3:
                    dve.wait_ge(attended, 4 * a + gi + 1)
                    for q in qs:
                        ins = d.bn_stats(st2[:, q, :], h1[:, q, :])
                    ins.then_inc(st2_done, 1)

            def ln2(a):
                dve.wait_ge(attended, 4 * a + 4)
                dve.wait_ge(st2_done, 3 * a + 3)
                after(dve, x2_upper, a)
                link = Link(dve, ch_ln2, a * N_LN, N_LN)
                norm(link, st2, h1, x2, GROUPS[-1], nw2, x2_scale).then_inc(x2_ready, 1)
                link.end()

            def router_logits(f):
                dve.wait_ge(logits, f + 1)
                link = Link(dve, ch_fin, f * N_FIN, N_FIN)
                link(d.tensor_tensor(lg[:], psO[:, 0:T * E].rearrange("p (t e) -> p t e", e=E),
                                     rb[:].unsqueeze(1).broadcast_to([P, T, E]), ALU.add))
                link(d.tensor_reduce(r6[:, 0, :], lg[:], AX.X, ALU.max))
                d.tensor_tensor(lg[:], lg[:], r6[:, 0, :].unsqueeze(2).broadcast_to([P, T, E]),
                                ALU.subtract).then_inc(lg_ready, 1)
                return link

            def wide(x):
                return x.unsqueeze(2).broadcast_to([P, T, E])

            def router_probs(f, link):
                dve.wait_ge(pr_ready, f + 1)
                link(d.tensor_reduce(r6[:, 1, :], pr[:], AX.X, ALU.add))
                link(d.reciprocal(r6[:, 2, :], r6[:, 1, :]))
                link(d.tensor_tensor(pr[:], pr[:], wide(r6[:, 2, :]), ALU.mult))

            def choose(link, n):
                left = (pr, lg)[n][:]
                link(d.tensor_reduce(r6[:, 3 + n, :], left, AX.X, ALU.max))
                link(d.tensor_tensor(sel[:, 0, :, :], left, wide(r6[:, 3 + n, :]), ALU.is_lt))
                link(d.scalar_tensor_tensor(sel[:, 0, :, :], sel[:, 0, :, :], float(E), iota16[:],
                                            ALU.mult, ALU.add))
                link(d.tensor_reduce(r6[:, 5 + n, :], sel[:, 0, :, :], AX.X, ALU.min))
                link(d.tensor_tensor(sel[:, 1 + n, :, :], iota16[:], wide(r6[:, 5 + n, :]), ALU.is_equal))
                if n == 0:
                    link(d.scalar_tensor_tensor(lg[:], sel[:, 1, :, :], -2.0, pr[:], ALU.mult, ALU.add))

            def choices(link):
                choose(link, 1)
                link(d.tensor_tensor(mask[:], sel[:, 1, :, :], sel[:, 2, :, :], ALU.add))
                d.tensor_scalar(mask[:, T - 1, :], mask[:, T - 1, :], valid[:], None, ALU.mult).then_inc(mask_ready, 1)
                link.end()

            def positions(f):
                link = Link(dve, ch_pos, f * N_POS, N_POS)
                dve.wait_ge(rank_psum, f + 1)
                d.tensor_reduce(cnt[:, 1, :], mask[:].rearrange("p t e -> p e t"), AX.X, ALU.add)
                dve.wait_ge(mask_ready, f + 1)
                d.tensor_tensor(tpos[:], psO[:, 0:T * E].rearrange("p (t e) -> p t e", e=E), eoff[:], ALU.add)\
                    .then_inc(rank_read, 1)
                dve.wait_ge(rank_read, f + 1)
                for k in range(2):
                    link(d.tensor_tensor(sel[:, 0, :, :], sel[:, 1 + k, :, :], tpos[:], ALU.mult))
                    link(d.tensor_reduce(pos[:, k, :], sel[:, 0, :, :], AX.X, ALU.add))
                last = pos[:, :, T - 1]
                link(d.tensor_scalar(last, last, valid[:], None, ALU.mult))
                link(d.tensor_tensor(last, last, spill[:], ALU.add))
                after(dve, scattered, 16 * 2 * T * f)
                d.tensor_scalar(posu[:], pos[:], 1.0, None, ALU.mult)
                link(d.tensor_scalar(spill[:], spill[:], invalid[:], None, ALU.add))
                d.tensor_copy(xrow[:, :, D], r6[:, 5, :])
                d.tensor_copy(xrow[:, :, D + 1:D + 3], r6[:, 3:5, :].rearrange("p a t -> p t a"))
                link(d.tensor_copy(xrow[:, :, D + 3], dest[:]))
                d.tensor_tensor(cnt[:, 0, :], cnt[:, 0, :], cnt[:, 1, :], ALU.add)
                link(d.tensor_scalar(dest[:], dest[:], float(STEPS), None, ALU.add))
                link.end()
                d.tensor_copy(pos[:, 0, 0:1], pos[:, 0, 0:1]).then_inc(pos_ready, 1)

            def body(b, tok, att, fin):
                a, f = b - 1, b - 2
                if tok:
                    after(dve, loc3_ready, T * b + 2)
                    after(dve, dy_ready, T * b)
                    d.tensor_copy(v_cur[:], v_nxt[:]).then_inc(v_cur_ready, 1)
                    dve.wait_ge(v_cur_ready, b + 1)
                link = None
                for i in range(T):
                    if tok:
                        if i + 1 < T:
                            lo_of(b, i + 1)
                        if i + 2 < T:
                            inc3_of(b, i + 2, v_cur)
                        if i >= 2:
                            dve.wait_ge(h_ready, T * b + i - 1)
                            d.bn_stats(st1[:, i - 2, :], hb[:, i - 2, :]).then_inc(st1_done, 1)
                        if i == 2:
                            inc2_of(b + 1)
                        if i == T - 1:
                            a2_of(b + 1)
                            inc3_of(b + 1, 0, v_nxt)
                            inc3_of(b + 1, 1, v_nxt)
                    if att and i == 0:
                        ln1(a)
                    if fin and i == 1:
                        router_probs(f, link)
                    if tok:
                        weigh(b, i, 0)
                    if fin and i == 1:
                        choose(link, 0)
                    if att and i == 1:
                        k_copy(a)
                    if fin and i == 1:
                        choices(link)
                    if fin and i == 2:
                        positions(f)
                    if tok:
                        weigh(b, i, 1)
                    if fin and i == 0:
                        link = router_logits(f)
                    if att and i >= 1:
                        if i >= 2:
                            attend(a, i - 2)
                        if i - 1 < 4:
                            negmax_of(a, i - 1)
                if tok:
                    lo_of(b + 1, 0)
                if att:
                    ln2(a)

            inc2_of(0)
            a2_of(0)
            inc3_of(0, 0, v_nxt)
            inc3_of(0, 1, v_nxt)
            lo_of(0, 0)
            for k in range(6):
                dve.wait_ge(w_hi, k + 1)
                d.tensor_tensor(w4l[:, k, :], wstage[k], w4h[:, k, :].bitcast(F32),
                                ALU.subtract).then_inc(w_split, 1)
            dve.wait_ge(w_split, 6)
            d.tensor_copy(w4l[64:96, 5, :], w4h[64:96, 5, :].bitcast(F32)).then_inc(w_split, 1)

            body(0, True, False, False)
            body(1, True, True, False)
            with dve.Fori(2, B) as b:
                body(b, True, True, True)
            body(B, False, True, True)
            last = router_logits(B - 1)
            router_probs(B - 1, last)
            choose(last, 0)
            choices(last)
            positions(B - 1)

            link = Link(dve, ch_tab, 0, 12)
            dve.wait_ge(counts, 1)
            link(d.tensor_scalar(tiles_i[0:E, :], psO[0:E, 0:1], 1.0 / SLOT, (SLOT - 1) / SLOT - 0.5 + 0.5 / SLOT,
                                 ALU.mult, ALU.add))
            d.tensor_copy(tiles_f[0:E, 0:1], tiles_i[0:E, :]).then_inc(tiles_ready, 1)
            link(d.tensor_tensor(fillrow[:], psS[:, 0:E], eoff[:, 0, :], ALU.add))
            dve.wait_ge(tiles_sum, 1)
            link(d.tensor_copy(tiles_f[0:E, 1:2], psO[0:E, 16:17]))
            link(d.tensor_scalar(ind[0:E, 0, :], iotaj[0:E, :], tiles_f[0:E, 1:2], None, ALU.is_ge))
            d.tensor_scalar(ind[0:E, 1, :], ind[0:E, 0, :], tiles_f[0:E, 0:1], None, ALU.mult).then_inc(ind_ready, 1)
            dve.wait_ge(slot_sum, 1)
            link(d.scalar_tensor_tensor(slot_f[:, 1, :], psS[:, SLOTX:2 * SLOTX], -1.0, iotaj[:], ALU.mult, ALU.add))
            link(d.tensor_scalar(slot_f[:, 0, :], psS[:, 0:SLOTX], float(REGION / SLOT), None, ALU.mult))
            link(d.tensor_tensor(slot_f[:, 1, :], slot_f[:, 1, :], slot_f[:, 0, :], ALU.add))
            d.tensor_scalar(slot_i[:, 1, :], slot_f[:, 1, :], float(SLOT), float(DUMMY), ALU.mult, ALU.min)
            link(d.scalar_tensor_tensor(slot_f[:, 2, :], psS[:, 0:SLOTX], float(E), iotaj[:], ALU.is_equal, ALU.mult))
            link(d.tensor_tensor(slot_f[:, 2, :], slot_f[:, 2, :], psS[:, SLOTX:2 * SLOTX], ALU.max))
            link(d.tensor_scalar(slot_f[:, 0, :], psS[:, 0:SLOTX], float(E - 1), None, ALU.min))
            for k in range(RING):
                ins = d.tensor_scalar(seen_i[:, k, :], slot_f[:, 2, :], float(RING - 1 - k), 32.0 / RING, ALU.add, ALU.mult)
            link(ins)
            link(d.tensor_scalar(seen_i[:], seen_i[:], -32, 16, ALU.bitwise_and, ALU.bitwise_or))
            link.end()
            d.tensor_copy(slot_i[:, 0, :], slot_f[:, 0, :]).then_inc(table, 1)
            dve.wait_ge(table, 1)

            def w1_of(j, u, ex):
                after(dve, up, 2 * j - 2)
                after(dve, gelu, j - 1)
                d.tensor_scalar(b1c[:, u, :], b1_all_e[:, bass.ds(ex, 1), :].rearrange("p a c -> p (a c)"), 1.0, None, ALU.mult)
                d.tensor_scalar(w1c[u], w1_all[:, bass.ds(ex, 1), :].rearrange("p a f -> p (a f)"), 1.0, None,
                                ALU.mult).then_inc(w1_ready, 1)

            def meta_of(j, u, k, n):
                rows = xg[:, k, :].rearrange("p (s c) -> p s c", s=2)
                ev = slot_f[:, 0, j:j + 1] if isinstance(j, int) else slot_f[:, 0, bass.ds(j, 1)]
                if not isinstance(n, int) or n > 0:
                    dve.wait_ge(added[k], 16 + 32 * n)
                after(dve, y_ready, j - 1)
                link = Link(dve, ch_meta, j * 1, 1)
                d.scalar_tensor_tensor(gtmp[:, u, 0, :], rows[:, :, D], ev, rows[:, :, D + 1], ALU.is_equal, ALU.mult)
                link(d.scalar_tensor_tensor(gtmp[:, u, 1, :], rows[:, :, D], ev, rows[:, :, D + 2], ALU.not_equal, ALU.mult))
                d.tensor_copy(destu[:, k, :], rows[:, :, D + 3])
                d.tensor_tensor(gate[:, u, :], gtmp[:, u, 0, :], gtmp[:, u, 1, :], ALU.add).then_inc(meta_ready, 1)
                link.end()

            def y_of(j, u, k, ex):
                dve.wait_ge(down, j + 1)
                dve.wait_ge(meta_ready, j + 1)
                link = Link(dve, ch_y, j, 1)
                b2e = b2_all[:, bass.ds(ex * D, D)].unsqueeze(1).broadcast_to([P, 2, D])
                yy = yr[:, k, :].rearrange("p (s d) -> p s d", s=2)
                link(d.tensor_tensor(yy, psY[u].rearrange("p (s d) -> p s d", s=2), b2e, ALU.add))
                for s in range(2):
                    ins = d.tensor_scalar(yy[:, s, :], yy[:, s, :], gate[:, u, s:s + 1], None, ALU.mult)
                ins.then_inc(y_ready, 1)
                link.end()

            def expert_of(j):
                return dve.value_load(slot_i[0:1, 0, j:j + 1] if isinstance(j, int) else slot_i[0:1, 0, bass.ds(j, 1)],
                                      min_val=0, max_val=E - 1)

            def slot(j, u, k, n):
                e1_ = expert_of(j + 1)
                w1_of(j + 1, 1 - u, e1_)
                dve.wait_ge(xg_in[k], 16 * (n + 1))
                meta_of(j, u, k, n)
                if not isinstance(j, int) or j > 0:
                    y_of(j - 1, 1 - u, (k - 1) % RING, expert_of(j - 1))

            dve.wait_ge(wl, 32)
            dve.wait_ge(wl2, 32)
            w1_of(0, 0, expert_of(0))
            for j in range(6):
                slot(j, j % 2, j % 4, j // 4)
            with dve.Fori(0, (SLOTS - 6) // 4) as n:
                for k in range(4):
                    slot(n * 4 + 6 + k, k % 2, (k + 2) % 4, n + 1 + (k + 2) // 4)
            y_of(SLOTS - 1, 1, (SLOTS - 1) % RING, expert_of(SLOTS - 1))

        @block.tensor
        def _(pe):
            t_ = nc.tensor
            pe.wait_ge(consts, N_CONST)

            def s2_of(b):
                pe.wait_ge(inc2_ready, b + 1)
                pe.wait_ge(run2_ready, b + 1)
                after(pe, h_ready, T * (b - 1) + 4)
                o = psS[:, 0:T * 64]
                t_.matmul(o, before[:, 0:P], inc2[:].rearrange("p t n -> p (t n)"), start=True, stop=False)
                t_.matmul(o, ones[:], run2[:].rearrange("p t n -> p (t n)"), start=False, stop=True)\
                    .then_inc(s2_sum, 1)

            def a3_of(b, i):
                pe.wait_ge(inc3_ready, T * b + i + 1)
                pe.wait_ge(loc3_ready, T * b + i + 1)
                after(pe, a3_lo, 2 * T * b + 2 * i)
                for k in range(4):
                    o = psA[:, k // 2, (k % 2) * 129:(k % 2) * 129 + 129]
                    t_.matmul(o, inc3[:, i % 2, k * P:(k + 1) * P], before[:], start=True, stop=False)
                    ins = t_.matmul(o[:, 0:P], loc3[:, i % 2, k * P:(k + 1) * P], ident[:], is_transpose=True,
                                    start=False, stop=True)
                    if k % 2:
                        ins.then_inc(a3_sum, 1)

            def pack_of(b, i):
                pe.wait_ge(a2_ready, b + 1)
                after(pe, h_ready, T * b + (-1, 0, 0, 1, 2, 3)[i])
                after(pe, pack_copied, T * b + i)
                t_.transpose(psS[:, 0:P], pack[:, i, 0:P], ident[:])
                t_.transpose(psS[:, P:2 * P], pack[:, i, P:2 * P], ident[:]).then_inc(pack_sum, 1)

            def main_of(b, i, h):
                after(pe, weighed, LH * (2 * T * b + 2 * i + h - 1))
                if h == 0:
                    pe.wait_ge(a3_lo, 2 * T * b + 2 * i + 2)
                    pe.wait_ge(pack_copied, T * b + i + 1)
                o = psP[:, h, :]
                cols = slice(h * 512, h * 512 + 512)
                first = True
                start = isinstance(b, int) and T * b + i + h == 0
                for k in range(4):
                    if start:
                        pe.wait_ge(w_split, k + 1)
                    hi, lo = (x[:, i % 2, k * P:(k + 1) * P] for x in (a3h, a3l))
                    for left, right in ((lo, w4h), (hi, w4l), (hi, w4h)):
                        t_.matmul(o, left, right[:, k, cols], start=first, stop=False)
                        first = False
                if start:
                    pe.wait_ge(w_split, 7)
                t_.matmul(o, packT[:, i % 2, P:2 * P], w4l[:, 5, cols], start=False, stop=False)
                t_.matmul(o, packT[:, i % 2, 0:P], w4h[:, 4, cols], start=False, stop=True)\
                    .then_inc(main_done, 1)

            def path_of(b, i):
                pe.wait_ge(dy_ready, T * b + i + 1)
                if i >= 1:
                    pe.wait_ge(h_ready, T * b + i)
                if i <= 3:
                    pe.wait_ge(pack_copied, T * b + i + 3)
                elif i == 4:
                    pe.wait_ge(s2_read, b + 2)
                else:
                    pe.wait_ge(pack_copied, T * (b + 1) + 1)
                o = psS[:, 0:P]
                t_.matmul(o, upto[:], dy[:, i % 2, :], start=True, stop=False)
                left, right = (ones[:], bias0[:]) if i == 0 else (last_row[:], hb[:, i - 1, :])
                t_.matmul(o, left, right, start=False, stop=True).then_inc(path_sum, 1)

            def x1T_of(a):
                pe.wait_ge(x1_ready, a + 1)
                pe.wait_ge(x1_upper, a + 1)
                for i in range(T):
                    ins = t_.transpose(psW[:, i * P:(i + 1) * P], x1[:, i, :], ident[:])
                ins.then_inc(x1T_psum, 1)

            def k_of(a):
                pe.wait_ge(x1T_ready, a + 1)
                after(pe, lg_ready, a)
                t_.matmul(psW[:, 0:512], waT[:], x1T[:, 0:512], start=True, stop=True)
                t_.matmul(psW[:, 512:768], waT[:], x1T[:, 512:768], start=True, stop=True)
                for i in range(T):
                    o = psO[:, i * D:(i + 1) * D] if i < 4 else psW[:, (i + 2) * D:(i + 3) * D]
                    ins = t_.matmul(o, x1T[:, i * P:(i + 1) * P], waT[:], start=True, stop=True)
                ins.then_inc(k_psum, 1)

            def scores_of(a, gi):
                if gi == 0:
                    pe.wait_ge(k_ready, a + 1)
                    pe.wait_ge(k_ready2, a + 1)
                else:
                    pe.wait_ge(pT_ready, 4 * a + gi)
                for q in GROUPS[gi]:
                    base, n = PLACE[q], q * P
                    left = x1T[:, q * P:(q + 1) * P]
                    for c0 in range(0, n, 512):
                        c1 = min(c0 + 512, n)
                        t_.matmul(psW[:, base + c0:base + c1], left, kT[:, c0:c1], start=True, stop=True)
                    o = psW[:, base + n:base + n + P]
                    t_.matmul(o, left, kT[:, n:n + P], start=True, stop=False)
                    ins = t_.matmul(o, ident16[:], future[:], start=False, stop=True)
                ins.then_inc(scores, 1)

            def pT_of(a, gi):
                pe.wait_ge(exp_ready, 4 * a + gi + 1)
                for q in GROUPS[gi]:
                    for k in range(q + 1):
                        c = PLACE[q] + k * P
                        ins = t_.transpose(psW[:, c:c + P], probs[:, c:c + P], ident[:])
                ins.then_inc(pT_psum, 1)

            def pv_of(a, gi):
                pe.wait_ge(pT_ready, 4 * a + gi + 1)
                if gi == 0:
                    pe.wait_ge(k_ready2, a + 1)
                    after(pe, rank_read, a)
                else:
                    pe.wait_ge(attended, 4 * a + gi)
                for s, q in enumerate(GROUPS[gi]):
                    for k in range(q + 1):
                        c = PLACE[q] + k * P
                        ins = t_.matmul(psO[:, s * D:(s + 1) * D], probsT[:, c:c + P], kk[:, k, :],
                                        start=(k == 0), stop=(k == q))
                ins.then_inc(pv_psum, 1)

            def x2T_of(f):
                pe.wait_ge(x2_ready, f + 1)
                pe.wait_ge(x2_upper, f + 1)
                for i in range(T):
                    ins = t_.transpose(psW[:, i * P:(i + 1) * P], x2[:, i, :], ident[:])
                ins.then_inc(x2T_psum, 1)

            def logits_of(f):
                pe.wait_ge(x2T_ready, f + 1)
                pe.wait_ge(attended, 4 * f + 4)
                for i in range(T):
                    ins = t_.matmul(psO[:, i * E:(i + 1) * E], x2T[:, i * P:(i + 1) * P], rwT[:],
                                    start=True, stop=True)
                ins.then_inc(logits, 1)

            def rank_of(f):
                pe.wait_ge(mask_ready, f + 1)
                o = psO[:, 0:T * E]
                t_.matmul(o, before[:, 0:P], mask[:].rearrange("p t e -> p (t e)"), start=True, stop=False)
                for i in range(T - 1):
                    t_.matmul(psO[:, (i + 1) * E:T * E], ones[:],
                              mask[:, i, :].unsqueeze(1).broadcast_to([P, T - 1 - i, E]), start=False, stop=False)
                t_.matmul(o, ones[:], cnt[:, 0, :].unsqueeze(1).broadcast_to([P, T, E]), start=False, stop=True)\
                    .then_inc(rank_psum, 1)

            def body(b, tok, att, fin):
                a, f = b - 1, b - 2
                if att:
                    path_of(a, T - 1)
                for i in range(T):
                    if tok:
                        if i + 1 < T:
                            pack_of(b, i + 1)
                            a3_of(b, i + 1)
                        else:
                            s2_of(b + 1)
                        main_of(b, i, 0)
                        if i >= 1:
                            path_of(b, i - 1)
                    if fin and i == 0:
                        x2T_of(f)
                    if att:
                        if i == 1:
                            k_of(a)
                        if i >= 2:
                            pT_of(a, i - 2)
                    if fin and i == 2:
                        rank_of(f)
                    if tok:
                        main_of(b, i, 1)
                    if fin and i == 0:
                        logits_of(f)
                    if att:
                        if i == 0:
                            x1T_of(a)
                        if i >= 2:
                            pv_of(a, i - 2)
                        if 1 <= i < 5:
                            scores_of(a, i - 1)
                if tok:
                    pack_of(b + 1, 0)
                    a3_of(b + 1, 0)

            pe.wait_ge(ld, 16 * 7)
            s2_of(0)
            pack_of(0, 0)
            a3_of(0, 0)
            body(0, True, False, False)
            body(1, True, True, False)
            with pe.Fori(2, B) as b:
                body(b, True, True, True)
            body(B, False, True, True)
            x2T_of(B - 1)
            logits_of(B - 1)

            rank_of(B - 1)
            pe.wait_ge(pos_ready, B)
            t_.matmul(psS[:, 0:E], ones[:], cnt[:, 0, :], start=True, stop=True)
            t_.matmul(psO[0:E, 0:1], cnt[:, 0, :], ones[:, 0:1], start=True, stop=True).then_inc(counts, 1)
            pe.wait_ge(tiles_ready, 1)
            t_.matmul(psO[0:E, 16:17], upto[0:E, 0:E], tiles_f[0:E, 0:1], start=True, stop=True).then_inc(tiles_sum, 1)
            pe.wait_ge(ind_ready, 1)
            t_.matmul(psS[:, 0:2 * SLOTX], ones[0:E, :], ind[0:E, :, :].rearrange("p a j -> p (a j)"),
                      start=True, stop=True).then_inc(slot_sum, 1)

            def xT_of(j, u, k, n):
                pe.wait_ge(xg_in[k], 16 * (n + 1))
                after(pe, xT_ready, j)
                for s in range(2):
                    ins = t_.transpose(psX[:, s * P:(s + 1) * P], xg[:, k, s * ROW:s * ROW + D], ident[:])
                ins.then_inc(xT_psum, 1)

            def up_of(j, u):
                pe.wait_ge(xT_ready, j + 1)
                pe.wait_ge(w1_ready, j + 1)
                after(pe, gelu, j - 1)
                for c in range(4):
                    ins = t_.matmul(psH[u][:, c * SLOT:(c + 1) * SLOT], w1c[u][:, c * P:(c + 1) * P], xTc[u],
                                    start=True, stop=True)
                    if c % 2:
                        ins.then_inc(up, 1)

            def down_of(j, u, ex):
                pe.wait_ge(gelu, j + 1)
                after(pe, y_ready, j - 1)
                for s in range(2):
                    for c in range(4):
                        ins = t_.matmul(psY[u][:, s * D:(s + 1) * D], hTc[:, u, c, s * P:(s + 1) * P],
                                        w2_all[:, bass.ds(ex * 4 + c, 1), :].rearrange("p a d -> p (a d)"),
                                        start=(c == 0), stop=(c == 3))
                ins.then_inc(down, 1)

            def expert_of(j):
                return pe.value_load(slot_i[0:1, 0, j:j + 1] if isinstance(j, int) else slot_i[0:1, 0, bass.ds(j, 1)],
                                     min_val=0, max_val=E - 1)

            def slot(j, u, k1, n1):
                up_of(j, u)
                xT_of(j + 1, 1 - u, k1, n1)
                if not isinstance(j, int) or j > 0:
                    down_of(j - 1, 1 - u, expert_of(j - 1))

            pe.wait_ge(table, 1)
            pe.wait_ge(wl2, 32)
            xT_of(0, 0, 0, 0)
            for j in range(6):
                slot(j, j % 2, (j + 1) % 4, (j + 1) // 4)
            with pe.Fori(0, (SLOTS - 6) // 4) as n:
                for k in range(4):
                    slot(n * 4 + 6 + k, k % 2, (k + 3) % 4, n + 1 + (k + 3) // 4)
            down_of(SLOTS - 1, 1, expert_of(SLOTS - 1))


def kernel(x, L0_tok_W, L0_tok_b, L0_attn_W, L0_ffn_router_w, L0_ffn_router_b, L0_ffn_w1, L0_ffn_b1,
           L0_ffn_w2, L0_ffn_b2):
    import numpy as np
    import concourse.bacc as bacc
    from concourse.bass_utils import run_bass_kernel_spmd

    f32 = np.float32
    x = np.asarray(x)
    n = STEPS + 1
    time = np.arange(n, dtype=f32) * f32(1.0 / STEPS)
    time[-1] = 1.0
    path = np.concatenate([np.broadcast_to(time[:, None, None], (n, B, 1)), x.transpose(1, 0, 2)], axis=2)
    path = np.pad(path, ((0, T * P + 1 - n), (0, 0), (0, 0)), mode="edge")

    def tiles(a):
        return np.ascontiguousarray(a.reshape(T, P, B, C).transpose(1, 2, 0, 3).reshape(P, B * T * C))

    W = np.asarray(L0_tok_W)
    W1t, W2t, W3t, W4t = (W[:, lo:lo + C ** k].T.reshape(-1, C * D)
                          for k, lo in ((1, 0), (2, C), (3, C + C ** 2), (4, C + C ** 2 + C ** 3)))
    gap = np.zeros((15, C * D), f32)
    w3y = np.concatenate([W3t, W2t, W2t, W1t, gap, W2t, W1t, np.zeros((23, C * D), f32)])
    w1 = np.asarray(L0_ffn_w1).transpose(0, 2, 1)
    w2 = np.asarray(L0_ffn_w2).transpose(0, 2, 1).reshape(E, FF // P, P, D).transpose(0, 2, 1, 3)
    arrays = {
        "xa": tiles(path[:-1]), "xb": tiles(path[1:]), "x0": path[0].reshape(1, B * C),
        "w4": W4t, "w3x": np.concatenate([W3t, W3t]), "w3y": w3y, "tok_b": np.asarray(L0_tok_b)[None],
        "attn_w": np.asarray(L0_attn_W).T, "router_w": np.asarray(L0_ffn_router_w).T,
        "router_b": np.asarray(L0_ffn_router_b)[None],
        "w1": w1, "b1": np.asarray(L0_ffn_b1).reshape(E, FF // P, P).transpose(0, 2, 1),
        "w2": w2, "b2": np.asarray(L0_ffn_b2),
    }
    arrays = {k: np.ascontiguousarray(a) for k, a in arrays.items()}
    nc = bacc.Bacc("TRN2", target_bir_lowering=False, num_devices=1)
    aps = {k: nc.dram_tensor(k, a.shape, mybir.dt.from_np(a.dtype), kind="ExternalInput").ap()
           for k, a in arrays.items()}
    out = nc.dram_tensor("out", (OUT_ROWS + SLOT, D), F32, kind="ExternalOutput").ap()
    build(nc, out=out, **aps)
    return run_bass_kernel_spmd(nc, [arrays], core_ids=[0]).results[0]["out"][:OUT_ROWS].reshape(B, STEPS, D)
```

```python
from contextlib import ExitStack

import concourse.bass as bass
from concourse import mybir

F32 = mybir.dt.float32
F32R = mybir.dt.float32r
BF16 = mybir.dt.bfloat16
U32 = mybir.dt.uint32
ALU = mybir.AluOpType
ACT = mybir.ActivationFunctionType
AX = mybir.AxisListType

P = 128
B = 16
STEPS = 749
T = 6
LAST = STEPS - (T - 1) * P
C = 8
D = 128
E = 16
FF = 512
NORM_DVE = 4
LH = 4
EPS = 1e-5
MASKED = -1e30
SLOT = 256
REGION = 12288
ROW = D + 4
DUMMY = E * REGION
SPILL = DUMMY + SLOT
OUT_ROWS = B * STEPS
SLOTS = (2 * OUT_ROWS + E * (SLOT - 1)) // SLOT
RING = 4
PEEL = SLOTS % RING + RING
SLOTX = -(-(SLOTS + 1) // RING) * RING
assert OUT_ROWS + SLOT <= REGION
GROUPS = [[0, 1, 2], [3], [4], [5]]
PLACE = {0: 0, 2: P, 1: 4 * P, 3: 0, 4: 0, 5: 0}


def after(eng, sem, value):
    if not isinstance(value, int) or value > 0:
        eng.wait_ge(sem, value)


class Link:

    def __init__(self, eng, sem, base, per):
        self.eng, self.sem, self.base, self.per, self.n = eng, sem, base, per, 0

    def __call__(self, instruction):
        self.n += 1
        instruction.then_inc(self.sem, 1)
        self.eng.wait_ge(self.sem, self.base + self.n)

    def end(self):
        assert self.n == self.per, (self.n, self.per)


def build(nc, xa, xb, x0, w4, w3x, w3y, tok_b, attn_w, router_w, router_b, w1, b1, w2, b2, out):
    ctx = ExitStack()
    with ctx:
        def sb(name, shape, dt=F32):
            return ctx.enter_context(nc.sbuf_tensor(name, shape, dt))

        def sem(name):
            return ctx.enter_context(nc.semaphore(name))

        ident = sb("ident", [P, P])
        ones = sb("ones", [P, P])
        before = sb("before", [P, P + 1])
        upto = sb("upto", [P, P])
        last_row = sb("last_row", [P, P])
        ident16 = sb("ident16", [P, P], BF16)
        future = sb("future", [P, P], BF16)
        waT = sb("waT", [P, D])
        rwT = sb("rwT", [P, E])
        rb = sb("rb", [P, E])
        bias0 = sb("bias0", [P, D])
        iota16 = sb("iota16", [P, T, E])
        iotai = sb("iotai", [P, T, E], mybir.dt.int32)
        NB1 = B + 1
        xas = sb("xas", [P, B * T * C])
        xbs = sb("xbs", [P, B * T * C])
        x0s = sb("x0s", [P, B * C])
        v_all = sb("v_all", [P, NB1 * T * C])
        a1_all = sb("a1_all", [P, NB1 * T * C])
        b1_all = sb("b1_all", [P, NB1 * T * C])
        d1_all = sb("d1_all", [P, NB1 * T * C])
        v_cur = sb("v_cur", [P, T, C])
        v_nxt = sb("v_nxt", [P, T, C])
        inc2 = sb("inc2", [P, T, 64])
        run2 = sb("run2", [P, T, 64])
        t1 = sb("t1", [P, T, 64])
        t2 = sb("t2", [P, T, 64])
        a2 = sb("a2", [P, T, 64])
        c2 = sb("c2", [P, T, 64])
        pack = sb("pack", [P, T, 256])
        inc3 = sb("inc3", [P, 2, 512])
        loc3 = sb("loc3", [P, 2, 512])
        carry = sb("carry", [P, T + 1, 4])
        a3h = sb("a3h", [P, 2, 512], F32R)
        a3l = sb("a3l", [P, 2, 512], F32R)
        packT = sb("packT", [P, 2, 256], F32R)
        dyp = sb("dyp", [P, 2, D])
        dy = sb("dy", [P, 2, D])
        hb = sb("hb", [P, T, D])
        h1 = sb("h1", [P, T, D])
        x1 = sb("x1", [P, T, D])
        x1T = sb("x1T", [P, T * P])
        kT = sb("kT", [P, T * P])
        kk = sb("kk", [P, T, D])
        negmax = sb("negmax", [P, T])
        rowsum = sb("rowsum", [P, T])
        rinv = sb("rinv", [P, T])
        probs = sb("probs", [P, T * P])
        probsT = sb("probsT", [P, T * P])
        st1 = sb("st1", [P, T, 6])
        st2 = sb("st2", [P, T, 6])
        mhalf = sb("mhalf", [P, T])
        nw1 = sb("nw1", [P, 6, T])
        nw2 = sb("nw2", [P, 6, T])
        x2 = sb("x2", [P, T, D])
        x2T = sb("x2T", [P, T * P])
        lg = sb("lg", [P, T, E])
        pr = sb("pr", [P, T, E])
        sel = sb("sel", [P, 3, T, E])
        r6 = sb("r6", [P, 7, T])
        valid = sb("valid", [P, 1])
        mask = sb("mask", [P, T, E])
        cnt = sb("cnt", [P, 2, E])
        eoff = sb("eoff", [P, T, E])
        eoffi = sb("eoffi", [P, T, E], mybir.dt.int32)
        tpos = sb("tpos", [P, T, E])
        pos = sb("pos", [P, 2, T])
        posu = sb("posu", [P, 2, T], U32)
        spill = sb("spill", [P, 2])
        spilli = sb("spilli", [P, 2], mybir.dt.int32)
        invalid = sb("invalid", [P, 1])
        dest = sb("dest", [P, T])
        desti = sb("desti", [P, T], mybir.dt.int32)
        xrow = sb("xrow", [P, T, ROW])
        fill = sb("fill", [P, 2, ROW])
        filli = sb("filli", [P, 2], mybir.dt.int32)
        w1_all = sb("w1_all", [P, E, FF])
        iotaj = sb("iotaj", [P, SLOTX])
        iotaji = sb("iotaji", [P, SLOTX], mybir.dt.int32)
        tiles_i = sb("tiles_i", [P, 1], mybir.dt.int32)
        tiles_f = sb("tiles_f", [P, 2])
        ind = sb("ind", [P, 2, SLOTX])
        slot_f = sb("slot_f", [P, 3, SLOTX])
        slot_i = sb("slot_i", [P, 2, SLOTX], mybir.dt.int32)
        seen_i = sb("seen_i", [P, RING, SLOTX], mybir.dt.int32)
        fillrow = sb("fillrow", [P, E], mybir.dt.int32)
        xg = sb("xg", [P, RING, 2 * ROW])
        gate = sb("gate", [P, 2, 2])
        gtmp = sb("gtmp", [P, 2, 2, 2])
        destu = sb("destu", [P, RING, 2], U32)
        biasc = sb("biasc", [P, RING, FF // P + D])
        xTl = sb("xTl", [P, 2, SLOT], F32R)
        yr = sb("yr", [P, RING, 2 * D])
        zero1 = sb("zero1", [P, 2])
        sorted_x = nc.dram_tensor("sorted_x", [SPILL + B * SLOT, ROW], F32).ap()
        first_count = nc.dram_tensor("first_count", [1, RING], F32).ap()
        wstage = [w1_all[:, 2 * k:2 * k + 2, :].rearrange("p e f -> p (e f)") for k in range(6)]
        w1h, w1l = a3h, a3l
        xTh = packT
        split_ctx = ExitStack()
        w4h = split_ctx.enter_context(nc.sbuf_tensor("w4h", [P, 6, 1024], F32R))
        w4l = split_ctx.enter_context(nc.sbuf_tensor("w4l", [P, 6, 1024], F32R))
        split_ctx.close()
        w2_all = sb("w2_all", [P, E * (FF // P), D])
        biases = sb("biases", [P, E, FF // P + D])
        hTc = sb("hTc", [P, 2, 4, SLOT])

        psP = ctx.enter_context(nc.psum_tensor("psP", [P, 2, 512], F32))
        psA = ctx.enter_context(nc.psum_tensor("psA", [P, 2, 512], F32))
        psS = ctx.enter_context(nc.psum_tensor("psS", [P, 512], F32))
        psO = ctx.enter_context(nc.psum_tensor("psO", [P, 512], F32))
        psW = ctx.enter_context(nc.psum_tensor("psW", [P, 1024], F32))
        psH = [psP[:].rearrange("p a b -> p (a b)"), psA[:].rearrange("p a b -> p (a b)")]
        psX, psY = psS, [psO[:, 0:2 * D], psW[:, 0:2 * D]]

        path_in, ld = sem("path_loaded"), sem("loaded_small")
        ldw = [sem(f"loaded_w{k}") for k in range(6)]
        w_split = sem("w_split")
        w_hi = sem("w_hi")
        consts = sem("consts")
        pchain = sem("pool_chain")
        paths = sem("paths")
        inc2_ready, run2_ready, s2_sum = sem("inc2_ready"), sem("run2_ready"), sem("s2_sum")
        a2_ready, s2_read, a2_upper = sem("a2_ready"), sem("s2_read"), sem("a2_upper")
        inc3_ready, loc3_ready = sem("inc3_ready"), sem("loc3_ready")
        a3_sum, a3_hi, a3_lo = sem("a3_sum"), sem("a3_hi"), sem("a3_lo")
        pack_sum, pack_copied = sem("pack_sum"), sem("pack_copied")
        main_done, weighed, dy_ready = sem("main_done"), sem("weighed"), sem("dy_ready")
        path_sum, h_ready = sem("path_sum"), sem("h_ready")
        ch_pre, ch_run2, ch_setup = sem("ch_pre"), sem("ch_run2"), sem("ch_setup")
        h_saved, x1_ready, x1T_psum, x1T_ready = sem("h_saved"), sem("x1_ready"), sem("x1T_psum"), sem("x1T_ready")
        k_psum, k_ready, k_ready2 = sem("k_psum"), sem("k_ready"), sem("k_ready2")
        scores, negmax_ready, exp_ready = sem("scores"), sem("negmax_ready"), sem("exp_ready")
        pT_psum, pT_ready, pv_psum, attended = sem("pT_psum"), sem("pT_ready"), sem("pv_psum"), sem("attended")
        x1_scale, x1_upper, x2_scale, x2_upper = sem("x1_scale"), sem("x1_upper"), sem("x2_scale"), sem("x2_upper")
        x1_var, x1_power, x2_var, x2_power = sem("x1_var"), sem("x1_power"), sem("x2_var"), sem("x2_power")
        ch_ln1, ch_ln2, ch_att = sem("ch_ln1"), sem("ch_ln2"), sem("ch_att")
        x2_ready, x2T_psum, x2T_ready, logits = sem("x2_ready"), sem("x2T_psum"), sem("x2T_ready"), sem("logits")
        lg_ready, pr_ready = sem("lg_ready"), sem("pr_ready")
        ch_fin = sem("ch_fin")
        h_stored = sem("h_stored")
        mask_ready, rank_psum, rank_read, pos_ready, xrow_ready, scattered = (
            sem("mask_ready"), sem("rank_psum"), sem("rank_read"), sem("pos_ready"), sem("xrow_ready"), sem("scattered"))
        ch_pos = sem("ch_pos")
        counts, tiles_ready, tiles_sum, ind_ready, slot_sum, table = (
            sem("counts"), sem("tiles_ready"), sem("tiles_sum"), sem("ind_ready"), sem("slot_sum"), sem("table"))
        ch_tab = sem("ch_tab")
        filled = sem("filled")
        wl, wl2 = sem("w1_loaded"), sem("w2_loaded")
        xg_in = [sem(f"xg_in{k}") for k in range(RING)]
        xT_psum, xT_hi, xT_ready, w1_hi, w1_ready, up, gelu, down = (
            sem("xT_psum"), sem("xT_hi"), sem("xT_ready"), sem("w1_hi"), sem("w1_ready"), sem("up"), sem("gelu_done"), sem("down"))
        meta_ready, y_sum, y_ready, y_seen = sem("meta_ready"), sem("y_sum"), sem("y_ready"), sem("y_seen")
        added = [sem(f"added{k}") for k in range(RING)]
        ch_meta = sem("ch_meta")
        st = sem("stored")
        rows_seen = sem("rows_seen")
        st1_done, st2_done = sem("st1_done"), sem("st2_done")
        v_cur_ready, ch_a2 = sem("v_cur_ready"), sem("ch_a2")

        block = ctx.enter_context(nc.Block())

        N_LN = 7
        N_PRE = 2
        N_FIN = 17
        N_POS = 9
        N_PC = 10
        N_CONST = 25 + 1

        @block.sync
        def _(sp):
            sp.dma_start(xas[:], xa).then_inc(path_in, 16)
            sp.dma_start(xbs[:], xb).then_inc(path_in, 16)
            sp.dma_start(x0s[:], x0.broadcast_to([P, B * C])).then_inc(path_in, 16)
            sp.dma_start(waT[:], attn_w).then_inc(ld, 16)
            sp.dma_start(rwT[:], router_w).then_inc(ld, 16)
            sp.dma_start(rb[:], router_b.broadcast_to([P, E])).then_inc(ld, 16)
            sp.wait_ge(pchain, N_PC)
            sp.dma_start(bias0[0:1, :], tok_b).then_inc(ld, 16)
            srcs = [w4[k * P:(k + 1) * P, :] for k in range(4)] + [w3x, w3y]
            for k, src in enumerate(srcs):
                sp.dma_start(wstage[k], src).then_inc(ldw[k], 16)

            sp.wait_ge(w_split, 6)
            sp.dma_start(w1_all[:], w1.rearrange("e p f -> p e f")).then_inc(wl, 16)
            sp.wait_ge(consts, N_CONST)
            sp.dma_start(out[OUT_ROWS:, :], fill[:, :, 0:D]).then_inc(st, 16)
            sp.dma_start(sorted_x[DUMMY:DUMMY + SLOT, :].rearrange("(p s) c -> p s c", s=2), fill[:]).then_inc(st, 16)

            def store(f):
                sp.wait_ge(attended, 4 * (f + 1))
                n = (T - 1) * P
                sp.dma_start(out[bass.ds(f * STEPS, n), :].rearrange("(t p) d -> p t d", p=P),
                             h1[:, 0:T - 1, :]).then_inc(h_stored, 16)
                sp.dma_start(out[bass.ds(f * STEPS + n, LAST), :], h1[0:LAST, T - 1, :]).then_inc(h_stored, 16)

            with sp.Fori(0, B) as f:
                store(f)

            sp.wait_ge(main_done, 2 * T * B)
            sp.wait_ge(w_split, 7)
            sp.dma_start(w2_all[:].rearrange("p (e c) d -> p e (c d)", e=E), w2.rearrange("e p c d -> p e (c d)")).then_inc(wl2, 16)
            sp.dma_start(biases[:, :, 0:FF // P], b1.rearrange("e p c -> p e c")).then_inc(wl2, 16)
            sp.dma_start(biases[:, :, FF // P:], b2.rearrange("(a e) d -> a e d", a=1).broadcast_to([P, E, D])).then_inc(wl2, 16)

            sp.wait_ge(table, 1)
            for e in range(0, E, 2):
                r = sp.value_load(fillrow[0:1, e:e + 1], min_val=0, max_val=DUMMY - SLOT)
                sp.dma_start(sorted_x[bass.ds(r, SLOT), :].rearrange("(p s) c -> p s c", s=2), fill[:])\
                    .then_inc(filled, 16)
            sp.wait_ge(filled, 16 * E)
            sp.wait_ge(scattered, 16 * 2 * T * B)
            sp.wait_ge(st, 32)
            sp.wait_ge(h_stored, 32 * B)

            def load_slot(j, k):
                after(sp, xT_psum, j - RING + 1)
                after(sp, meta_ready, j - RING + 1)
                r = sp.value_load(slot_i[0:1, 1, bass.ds(j, 1)] if not isinstance(j, int) else slot_i[0:1, 1, j:j + 1],
                                  min_val=0, max_val=DUMMY)
                sp.dma_start(xg[:, k, :], sorted_x[bass.ds(r, SLOT), :].rearrange("(p s) c -> p (s c)", s=2))\
                    .then_inc(xg_in[k], 16)

            for j in range(RING):
                load_slot(j, j)
            with sp.Fori(1, SLOTX // RING) as n:
                for k in range(RING):
                    load_slot(n * RING + k, k)
            for k in range(RING):
                sp.wait_ge(xg_in[k], 16 * (SLOTX // RING))
            for k in range(RING):
                sp.wait_ge(added[k], 16 + 32 * len(range(k, SLOTS, RING)))

        @block.gpsimd
        def _(pool):
            g = nc.gpsimd
            link = Link(pool, pchain, 0, N_PC)
            g.memset(ones[:], 1.0).then_inc(consts, 1)
            link(g.memset(bias0[:], 0.0))
            g.memset(v_all[:, B * T * C:], 0.0).then_inc(consts, 1)
            g.memset(a1_all[:, B * T * C:], 0.0).then_inc(consts, 1)
            g.memset(b1_all[:, B * T * C:], 0.0).then_inc(consts, 1)
            g.memset(d1_all[:, B * T * C:], 0.0).then_inc(consts, 1)
            g.memset(carry[:, 0, :], 0.0).then_inc(consts, 1)
            g.memset(run2[:, 0, :], 0.0).then_inc(consts, 1)
            link(g.memset(pack[:, :, 192:256], 0.0))
            g.memset(pack[:, :, 208:209], 1.0).then_inc(consts, 1)
            g.memset(pack[:, :, 232:233], 1.0).then_inc(consts, 1)
            link(g.memset(ident[:], 0.0))
            g.affine_select(out=ident[:], in_=ident[:], compare_op=ALU.not_equal, fill=1.0, base=0,
                            pattern=[[-1, P]], channel_multiplier=1).then_inc(consts, 1)
            link(g.memset(before[:], 1.0))
            g.affine_select(out=before[:], in_=before[:], compare_op=ALU.is_gt, fill=0.0, base=0,
                            pattern=[[1, P + 1]], channel_multiplier=-1).then_inc(consts, 1)
            link(g.memset(upto[:], 1.0))
            g.affine_select(out=upto[:], in_=upto[:], compare_op=ALU.is_ge, fill=0.0, base=0,
                            pattern=[[1, P]], channel_multiplier=-1).then_inc(consts, 1)
            link(g.memset(last_row[:], 1.0))
            g.affine_select(out=last_row[:], in_=last_row[:], compare_op=ALU.is_ge, fill=0.0, base=1 - P,
                            pattern=[[0, P]], channel_multiplier=1).then_inc(consts, 1)
            link(g.memset(ident16[:], 0.0))
            g.affine_select(out=ident16[:], in_=ident16[:], compare_op=ALU.not_equal, fill=1.0, base=0,
                            pattern=[[-1, P]], channel_multiplier=1).then_inc(consts, 1)
            link(g.memset(fill[:], 0.0))
            g.memset(mhalf[:], -0.5).then_inc(consts, 1)
            g.memset(zero1[:], 0.0).then_inc(consts, 1)
            g.memset(cnt[:, 0, :], 0.0).then_inc(consts, 1)
            link(g.memset(valid[:], 1.0))
            g.affine_select(out=valid[:], in_=valid[:], compare_op=ALU.is_gt, fill=0.0, base=LAST,
                            pattern=[[1, 1]], channel_multiplier=-1).then_inc(consts, 1)
            g.iota(eoffi[:], [[0, T], [REGION, E]], base=0, channel_multiplier=0).then_inc(consts, 1)
            g.iota(spilli[:], [[P, 2]], base=SPILL, channel_multiplier=1).then_inc(consts, 1)
            g.iota(desti[:], [[P, T]], base=0, channel_multiplier=1).then_inc(consts, 1)
            g.iota(filli[:], [[1, 2]], base=OUT_ROWS, channel_multiplier=2).then_inc(consts, 1)
            g.iota(iotaji[:], [[1, SLOTX]], base=0, channel_multiplier=0).then_inc(consts, 1)
            link(g.memset(future[:], MASKED))
            g.affine_select(out=future[:], in_=future[:], compare_op=ALU.is_gt, fill=0.0, base=0,
                            pattern=[[1, P]], channel_multiplier=-1).then_inc(consts, 1)
            g.iota(iotai[:], [[0, T], [1, E]], base=0, channel_multiplier=0).then_inc(consts, 1)
            link.end()
            pool.wait_ge(consts, N_CONST - 1)
            g.tensor_copy(fill[:, :, D + 3], filli[:]).then_inc(consts, 1)
            pool.wait_ge(consts, N_CONST)
            for k in range(RING):
                g.dma_start(first_count[:, k:k + 1], zero1[0:1, 0:1]).then_inc(added[k], 16)
            pool.wait_ge(paths, 4)

            def run2_of(b):
                pool.wait_ge(inc2_ready, b + 1)
                after(pool, s2_sum, b)
                link = Link(pool, ch_run2, b * (T - 2), T - 2)
                for i in range(T - 1):
                    ins = g.tensor_tensor(run2[:, i + 1, :], run2[:, i, :], inc2[:, i, :], ALU.add)
                    if i < T - 2:
                        link(ins)
                ins.then_inc(run2_ready, 1)
                link.end()

            def loc3_of(b, i, v):
                pool.wait_ge(s2_read, b + 1)
                after(pool, a3_sum, 2 * T * b + 2 * i - 2)
                g.tensor_tensor(loc3[:, i % 2, :].rearrange("p (a c) -> p a c", c=C),
                                c2[:, i, :].unsqueeze(2).broadcast_to([P, 64, C]),
                                v[:, i, :].unsqueeze(1).broadcast_to([P, 64, C]),
                                ALU.mult).then_inc(loc3_ready, 1)

            def power_of(n, var_ready, nw, power):
                pool.wait_ge(var_ready, n + 1)
                g.tensor_tensor(nw[:, 3, :], nw[:, 2, :], mhalf[:], ALU.pow).then_inc(power, 1)

            def save_h(a):
                pool.wait_ge(h_ready, T * a + T)
                after(pool, x2_ready, a)
                after(pool, x2_upper, a)
                after(pool, h_stored, a * 32)
                g.tensor_tensor(h1[:], hb[:], carry[:, 0, 0:1].unsqueeze(2).broadcast_to([P, T, D]), ALU.add)\
                    .then_inc(h_saved, 1)

            def scatter(f, i):
                for k in range(2):
                    g.indirect_dma_start(out=sorted_x, out_offset=bass.IndirectOffsetOnAxis(ap=posu[:, k, i:i + 1], axis=0),
                                         in_=xrow[:, i, :], in_offset=None).then_inc(scattered, 16)

            def rows_ready(f):
                pool.wait_ge(pos_ready, f + 1)
                pool.wait_ge(xrow_ready, f + 1)
                after(pool, rows_seen, f)
                g.tensor_tensor(zero1[:, 1:2], zero1[:, 0:1], zero1[:, 0:1], ALU.add).then_inc(rows_seen, 1)

            def body(b, tok, att, fin):
                if att:
                    power_of(b - 1, x1_var, nw1, x1_power)
                    save_h(b - 1)
                if tok:
                    pool.wait_ge(v_cur_ready, b + 1)
                for i in range(T):
                    if tok:
                        if i + 2 < T:
                            loc3_of(b, i + 2, v_cur)
                        if i == 2:
                            run2_of(b + 1)
                        if i == T - 1:
                            loc3_of(b + 1, 0, v_nxt)
                            loc3_of(b + 1, 1, v_nxt)
                    if fin and i == 4:
                        rows_ready(b - 2)
                        for m in range(4):
                            scatter(b - 2, m)
                    if fin and i == 5:
                        scatter(b - 2, 4)
                        scatter(b - 2, 5)
                if att:
                    power_of(b - 1, x2_var, nw2, x2_power)

            run2_of(0)
            loc3_of(0, 0, v_nxt)
            loc3_of(0, 1, v_nxt)
            body(0, True, False, False)
            body(1, True, True, False)
            with pool.Fori(2, B) as b:
                body(b, True, True, True)
            body(B, False, True, True)
            body(B + 1, False, False, True)

            def add_slot(j, k):
                cols = slice(j, j + 1) if isinstance(j, int) else bass.ds(j, 1)
                landed = [pool.value_load(seen_i[0:1, m, cols], min_val=16, max_val=16 + 32 * (SLOTS // RING + 1))
                          for m in range(RING)]
                pool.wait_ge(y_ready, j + 1)
                for m in range(RING):
                    pool.wait_ge(added[m], landed[m])
                after(pool, y_seen, j)
                g.tensor_tensor(zero1[:, 1:2], zero1[:, 0:1], zero1[:, 0:1], ALU.add).then_inc(y_seen, 1)
                for s in range(2):
                    g.indirect_dma_start(out=out, out_offset=bass.IndirectOffsetOnAxis(ap=destu[:, k, s:s + 1], axis=0),
                                         in_=yr[:, k, s * D:(s + 1) * D], in_offset=None,
                                         compute_op=ALU.add).then_inc(added[k], 16)

            pool.wait_ge(rows_seen, B)
            pool.wait_ge(table, 1)
            for j in range(PEEL):
                add_slot(j, j % RING)
            with pool.Fori(0, (SLOTS - PEEL) // RING) as n:
                for k in range(PEEL, PEEL + RING):
                    add_slot(n * RING + k, k % RING)

        @block.scalar
        def _(act):
            a_ = nc.scalar
            act.wait_ge(consts, N_CONST)

            def hi_of(b, i):
                for h in range(2):
                    act.wait_ge(a3_sum, 2 * T * b + 2 * i + h + 1)
                    if h == 0:
                        after(act, main_done, 2 * T * b + 2 * i - 2)
                        if i > 0:
                            act.wait_ge(a3_lo, 2 * T * b + 2 * i)
                    for k in (2 * h, 2 * h + 1):
                        ins = a_.activation(a3h[:, i % 2, k * P:(k + 1) * P],
                                            psA[:, h, (k % 2) * 129:(k % 2) * 129 + P],
                                            ACT.Identity, bias=carry[:, i, k:k + 1])
                    ins.then_inc(a3_hi, 1)

            def a2_upper_of(b):
                act.wait_ge(s2_read, b + 1)
                after(act, pack_sum, T * b)
                for c0 in (0, 128):
                    ins = a_.activation(pack[:, :, c0:c0 + 64].bitcast(F32R), a2[:], ACT.Copy)
                ins.then_inc(a2_upper, 1)

            def packT_of(b, i):
                act.wait_ge(pack_sum, T * b + i + 1)
                a_.activation(packT[:, i % 2, :], psS[:, 0:256], ACT.Copy).then_inc(pack_copied, 1)

            def h_of(b, i):
                act.wait_ge(path_sum, T * b + i + 1)
                if i == 0:
                    after(act, h_saved, b)
                    after(act, x1_ready, b)
                    after(act, x1_upper, b)
                a_.activation(hb[:, i, :], psS[:, 0:P], ACT.Copy).then_inc(h_ready, 1)

            def upper_of(n, scaled, src, dst, nw, done):
                act.wait_ge(scaled, n + 1)
                for i in range(NORM_DVE, T):
                    ins = a_.activation(dst[:, i, :], src[:, i, :], ACT.Identity, bias=nw[:, 5, i:i + 1],
                                        scale=nw[:, 3, i:i + 1])
                ins.then_inc(done, 1)

            def x1T_copy(a):
                act.wait_ge(x1T_psum, a + 1)
                a_.activation(x1T[:], psW[:, 0:T * P], ACT.Copy).then_inc(x1T_ready, 1)

            def k_copy(a):
                act.wait_ge(k_psum, a + 1)
                a_.activation(kT[:], psW[:, 0:T * P], ACT.Copy)
                a_.activation(kk[:, 4:6, :], psW[:, T * P:(T + 2) * P], ACT.Copy).then_inc(k_ready, 1)

            def exp_of(a, gi):
                act.wait_ge(negmax_ready, 4 * a + gi + 1)
                for q in GROUPS[gi]:
                    n = (q + 1) * P
                    ins = a_.activation(probs[:, PLACE[q]:PLACE[q] + n], psW[:, PLACE[q]:PLACE[q] + n],
                                        ACT.Exp, bias=negmax[:, q:q + 1], accum_out=rowsum[:, q:q + 1])
                ins.then_inc(exp_ready, 1)

            def pT_copy(a, gi):
                n = max(PLACE[q] + (q + 1) * P for q in GROUPS[gi])
                act.wait_ge(pT_psum, 4 * a + gi + 1)
                a_.activation(probsT[:, 0:n], psW[:, 0:n], ACT.Copy).then_inc(pT_ready, 1)

            def x2T_copy(f):
                for h, cols in enumerate((slice(0, 4 * P), slice(4 * P, T * P))):
                    act.wait_ge(x2T_psum, 2 * f + h + 1)
                    a_.activation(x2T[:, cols], psW[:, cols], ACT.Copy).then_inc(x2T_ready, 1)

            def xrow_copy(f):
                after(act, scattered, 16 * 2 * T * f)
                act.wait_ge(x2_ready, f + 1)
                act.wait_ge(x2_upper, f + 1)
                a_.activation(xrow[:, :, 0:D], x2[:], ACT.Copy).then_inc(xrow_ready, 1)

            def router_exp(f):
                act.wait_ge(lg_ready, f + 1)
                a_.activation(pr[:], lg[:], ACT.Exp).then_inc(pr_ready, 1)

            def body(b, tok, att, fin):
                a, f = b - 1, b - 2
                if att:
                    h_of(a, T - 1)
                for i in range(T):
                    if tok and i + 1 < T:
                        packT_of(b, i + 1)
                        hi_of(b, i + 1)
                    if i == 1 and fin:
                        router_exp(f)
                    if tok and i == T - 1:
                        a2_upper_of(b + 1)
                    if tok and i >= 1:
                        h_of(b, i - 1)
                    if i == 0 and fin:
                        upper_of(f, x2_scale, h1, x2, nw2, x2_upper)
                    if i == 0 and att:
                        upper_of(a, x1_scale, hb, x1, nw1, x1_upper)
                    if i == 0 and fin:
                        x2T_copy(f)
                    if i == 0 and att:
                        x1T_copy(a)
                    if i == 0 and fin:
                        xrow_copy(f)
                    if att:
                        if i == 1:
                            k_copy(a)
                            exp_of(a, 0)
                        if i >= 2:
                            pT_copy(a, i - 2)
                            if i - 1 < 4:
                                exp_of(a, i - 1)
                if tok:
                    packT_of(b + 1, 0)
                    hi_of(b + 1, 0)

            a2_upper_of(0)
            for k in range(6):
                act.wait_ge(ldw[k], 16)
                a_.activation(w4h[:, k, :], wstage[k], ACT.Copy).then_inc(w_hi, 1)
            packT_of(0, 0)
            hi_of(0, 0)
            body(0, True, False, False)
            body(1, True, True, False)
            with act.Fori(2, B) as b:
                body(b, True, True, True)
            body(B, False, True, True)
            upper_of(B - 1, x2_scale, h1, x2, nw2, x2_upper)
            x2T_copy(B - 1)
            xrow_copy(B - 1)
            router_exp(B - 1)

            act.wait_ge(table, 1)
            for e in range(1, E, 2):
                r = act.value_load(fillrow[0:1, e:e + 1], min_val=0, max_val=DUMMY - SLOT)
                act.dma_start(sorted_x[bass.ds(r, SLOT), :].rearrange("(p s) c -> p s c", s=2), fill[:])\
                    .then_inc(filled, 16)

            def xT_copy(j, u):
                act.wait_ge(xT_psum, j + 1)
                after(act, up, 2 * j - 2)
                a_.activation(xTh[:, u, :], psX[:, 0:SLOT], ACT.Copy).then_inc(xT_hi, 1)

            def gelu_of(j, u, k):
                act.wait_ge(w1_ready, j + 1)
                for c in range(4):
                    if c % 2 == 0:
                        act.wait_ge(up, 2 * j + c // 2 + 1)
                    ins = a_.activation(hTc[:, u, c, :], psH[u][:, c * SLOT:(c + 1) * SLOT], ACT.Gelu,
                                        bias=biasc[:, k, c:c + 1])
                ins.then_inc(gelu, 1)

            def gate_of(j, u, k):
                act.wait_ge(y_sum, j + 1)
                act.wait_ge(meta_ready, j + 1)
                for s in range(2):
                    ins = a_.activation(yr[:, k, s * D:(s + 1) * D], yr[:, k, s * D:(s + 1) * D], ACT.Copy,
                                        scale=gate[:, u, s:s + 1])
                ins.then_inc(y_ready, 1)

            xT_copy(0, 0)
            for j in range(PEEL):
                xT_copy(j + 1, (j + 1) % 2)
                gelu_of(j, j % 2, j % RING)
                if j > 0:
                    gate_of(j - 1, (j - 1) % 2, (j - 1) % RING)
            with act.Fori(0, (SLOTS - PEEL) // RING) as n:
                for k in range(PEEL, PEEL + RING):
                    j = n * RING + k
                    xT_copy(j + 1, (k + 1) % 2)
                    gelu_of(j, k % 2, k % RING)
                    gate_of(j - 1, (k - 1) % 2, (k - 1) % RING)
            gate_of(SLOTS - 1, (SLOTS - 1) % 2, (SLOTS - 1) % RING)

        @block.vector
        def _(dve):
            d = nc.vector
            dve.wait_ge(path_in, 16 * 3)
            n0 = B * T * C
            link = Link(dve, ch_setup, 0, 8)
            d.tensor_tensor(v_all[:, 0:n0], xbs[:], xas[:], ALU.subtract).then_inc(paths, 1)
            x0b = x0s[:].rearrange("p (b c) -> p b c", c=C).unsqueeze(2).broadcast_to([P, B, T, C])
            link(d.tensor_tensor(xas[:].rearrange("p (b t c) -> p b t c", t=T, c=C),
                                 xas[:].rearrange("p (b t c) -> p b t c", t=T, c=C), x0b, ALU.subtract))
            dve.wait_ge(paths, 1)
            d.scalar_tensor_tensor(a1_all[:, 0:n0], v_all[:, 0:n0], 0.5, xas[:], ALU.mult, ALU.add).then_inc(paths, 1)
            link(d.tensor_scalar(xbs[:], xas[:], 0.5, None, ALU.mult))
            d.scalar_tensor_tensor(b1_all[:, 0:n0], v_all[:, 0:n0], 1.0 / 6, xbs[:], ALU.mult, ALU.add).then_inc(paths, 1)
            link(d.tensor_scalar(xas[:], xas[:], 1.0 / 6, None, ALU.mult))
            d.scalar_tensor_tensor(d1_all[:, 0:n0], v_all[:, 0:n0], 1.0 / 24, xas[:], ALU.mult, ALU.add).then_inc(paths, 1)
            dve.wait_ge(paths, 4)
            dve.wait_ge(consts, N_CONST)
            link(d.tensor_copy(iota16[:], iotai[:]))
            d.tensor_copy(eoff[:], eoffi[:])
            d.tensor_copy(dest[:], desti[:])
            d.tensor_copy(iotaj[:], iotaji[:])
            link(d.tensor_copy(spill[:], spilli[:]))
            link(d.tensor_scalar(invalid[:], valid[:], -1.0, 1.0, ALU.mult, ALU.add))
            link(d.tensor_scalar(spill[:], spill[:], invalid[:], None, ALU.mult))
            link(d.tensor_scalar(invalid[:], invalid[:], float(SLOT), None, ALU.mult))
            link.end()
            def outer(out_, left, right, n, k):
                return d.tensor_tensor(out_, left.unsqueeze(n).broadcast_to(k),
                                       right.unsqueeze(n - 1).broadcast_to(k), ALU.mult)

            def inc2_of(b):
                cols = bass.ds(b * (T * C), T * C)
                flat = v_nxt[:].rearrange("p t c -> p (t c)")
                after(dve, loc3_ready, T * (b - 1) + 2)
                after(dve, s2_sum, b)
                link = Link(dve, ch_pre, b * N_PRE, N_PRE)
                link(d.tensor_scalar(flat, v_all[:, cols], 1.0, None, ALU.mult))
                k4 = [P, T, C, C]
                v4 = v_nxt[:].unsqueeze(2).broadcast_to(k4)
                for src, dst in ((a1_all, inc2), (b1_all, t1), (d1_all, t2)):
                    left = src[:, cols].rearrange("p (t c) -> p t c", c=C).unsqueeze(3).broadcast_to(k4)
                    ins = d.tensor_tensor(dst[:].rearrange("p t (i j) -> p t i j", j=C), left, v4, ALU.mult)
                    if dst is inc2:
                        ins.then_inc(inc2_ready, 1)
                link(ins)
                link.end()

            def a2_of(b):
                s2 = psS[:, 0:T * 64].rearrange("p (t n) -> p t n", n=64)
                dve.wait_ge(s2_sum, b + 1)
                after(dve, loc3_ready, T * b)
                after(dve, pack_sum, T * b)
                link = Link(dve, ch_a2, b, 1)
                d.scalar_tensor_tensor(c2[:], s2, 0.5, t2[:], ALU.mult, ALU.add)
                d.tensor_tensor(a2[:], s2, t1[:], ALU.add).then_inc(s2_read, 1)
                cols = bass.ds(b * (T * C), T * C)
                a1v = a1_all[:, cols].rearrange("p (t c) -> p t c", c=C)
                link(d.tensor_scalar(pack[:, :, 192:200].bitcast(F32R), a1v, 1.0, None, ALU.mult))
                d.tensor_tensor(pack[:, :, 200:208], a1v, pack[:, :, 192:200], ALU.subtract)
                d.tensor_copy(pack[:, :, 224:232], pack[:, :, 192:200])
                link.end()

            def packs_of(b):
                dve.wait_ge(a2_upper, b + 1)
                d.tensor_tensor(pack[:, :, 64:128], a2[:], pack[:, :, 0:64], ALU.subtract).then_inc(a2_ready, 1)

            def inc3_of(b, i, v):
                if isinstance(i, int) and i < 2:
                    dve.wait_ge(s2_read, b + 1)
                after(dve, a3_sum, 2 * T * b + 2 * i - 2)
                d.tensor_tensor(inc3[:, i % 2, :].rearrange("p (a c) -> p a c", c=C),
                                a2[:, i, :].unsqueeze(2).broadcast_to([P, 64, C]),
                                v[:, i, :].unsqueeze(1).broadcast_to([P, 64, C]),
                                ALU.mult).then_inc(inc3_ready, 1)

            def lo_of(b, i):
                for h in range(2):
                    dve.wait_ge(a3_hi, 2 * T * b + 2 * i + h + 1)
                    for k in (2 * h, 2 * h + 1):
                        d.scalar_tensor_tensor(a3l[:, i % 2, k * P:(k + 1) * P],
                                               psA[:, h, (k % 2) * 129:(k % 2) * 129 + P],
                                               carry[:, i, k:k + 1],
                                               a3h[:, i % 2, k * P:(k + 1) * P].bitcast(F32),
                                               ALU.add, ALU.subtract)
                    d.tensor_tensor(carry[:, i + 1, 2 * h:2 * h + 2], psA[:, h, P:P + 130:129],
                                    carry[:, i, 2 * h:2 * h + 2], ALU.add).then_inc(a3_lo, 1)

            def weigh(b, i, h):
                dve.wait_ge(main_done, 2 * T * b + 2 * i + h + 1)
                n0 = 2 * LH * (T * b + i)
                for m in range(LH):
                    n, blk = h * LH + m, psP[:, h, m * D:(m + 1) * D]
                    vl, part = v_cur[:, i, n:n + 1], dyp[:, m % 2, :]
                    if n == 0:
                        after(dve, dy_ready, T * b + i)
                    if n < 2:
                        ins = d.tensor_scalar(part, blk, vl, None, ALU.mult)
                    else:
                        dve.wait_ge(weighed, n0 + n - 1)
                        ins = d.scalar_tensor_tensor(part, blk, vl, part, ALU.mult, ALU.add)
                    ins.then_inc(weighed, 1)
                if h == 1:
                    after(dve, path_sum, T * b + i - 1)
                    dve.wait_ge(weighed, n0 + 2 * LH)
                    d.tensor_tensor(dy[:, i % 2, :], dyp[:, 0, :], dyp[:, 1, :], ALU.add).then_inc(dy_ready, 1)

            def var_of(n, chain, stats, src, rest, nw, var_ready):
                link = Link(dve, chain, n * N_LN, 4)
                for i in rest:
                    ins = d.bn_stats(stats[:, i, :], src[:, i, :])
                link(ins)
                me, m2e, mo, m2o = (stats[:, :, c] for c in (1, 2, 4, 5))
                mean, dif, var = (nw[:, c, :] for c in range(3))
                d.tensor_tensor(mean, me, mo, ALU.add)
                d.tensor_tensor(dif, me, mo, ALU.subtract)
                link(d.tensor_tensor(var, m2e, m2o, ALU.add))
                link(d.tensor_tensor(dif, dif, dif, ALU.mult))
                d.tensor_scalar(mean, mean, 0.5, None, ALU.mult)
                link(d.tensor_scalar(var, var, 1.0 / D, EPS, ALU.mult, ALU.add))
                link.end()
                d.scalar_tensor_tensor(var, dif, 0.25, var, ALU.mult, ALU.add).then_inc(var_ready, 1)

            def norm_of(n, chain, src, dst, nw, power, scaled, done):
                mean, var, y, t = (nw[:, c, :] for c in (0, 2, 3, 4))
                dve.wait_ge(power, n + 1)
                link = Link(dve, chain, n * N_LN + 4, N_LN - 4)
                link(d.scalar_tensor_tensor(t, y, -0.5, y, ALU.mult, ALU.mult))
                link(d.tensor_tensor(t, t, var, ALU.mult))
                link(d.scalar_tensor_tensor(y, t, 1.5, y, ALU.add, ALU.mult))
                link.end()
                d.scalar_tensor_tensor(nw[:, 5, :], mean, -1.0, y, ALU.mult, ALU.mult).then_inc(scaled, 1)
                for i in range(NORM_DVE):
                    ins = d.tensor_scalar(dst[:, i, :], src[:, i, :], nw[:, 0, i:i + 1], nw[:, 3, i:i + 1],
                                          ALU.subtract, ALU.mult)
                ins.then_inc(done, 1)

            def var1_of(a):
                dve.wait_ge(h_ready, T * a + T)
                dve.wait_ge(st1_done, (T - 2) * (a + 1))
                after(dve, x1_upper, a)
                var_of(a, ch_ln1, st1, hb, [T - 2, T - 1], nw1, x1_var)

            def var2_of(a):
                dve.wait_ge(attended, 4 * a + 4)
                dve.wait_ge(st2_done, 3 * a + 3)
                after(dve, x2_upper, a)
                var_of(a, ch_ln2, st2, h1, GROUPS[-1], nw2, x2_var)

            def x1_of(a):
                norm_of(a, ch_ln1, hb, x1, nw1, x1_power, x1_scale, x1_ready)

            def x2_of(a):
                norm_of(a, ch_ln2, h1, x2, nw2, x2_power, x2_scale, x2_ready)

            def k_copy(a):
                dve.wait_ge(k_psum, a + 1)
                d.tensor_copy(kk[:, 0:4, :], psO[:].rearrange("p (k e) -> p k e", e=D)).then_inc(k_ready2, 1)

            def negmax_of(a, gi):
                dve.wait_ge(scores, 4 * a + gi + 1)
                for q in GROUPS[gi]:
                    n = (q + 1) * P
                    ins = d.tensor_reduce(negmax[:, q:q + 1], psW[:, PLACE[q]:PLACE[q] + n], AX.X, ALU.max,
                                          negate=True)
                ins.then_inc(negmax_ready, 1)

            def attend(a, gi):
                dve.wait_ge(exp_ready, 4 * a + gi + 1)
                qs = GROUPS[gi]
                link = Link(dve, ch_att, (4 * a + gi) * 2, 2)
                link(d.reciprocal(rinv[:, qs[0]:qs[-1] + 1], rowsum[:, qs[0]:qs[-1] + 1]))
                dve.wait_ge(pv_psum, 4 * a + gi + 1)
                for s, q in enumerate(qs):
                    ins = d.scalar_tensor_tensor(x1[:, q, :], psO[:, s * D:(s + 1) * D], rinv[:, q:q + 1],
                                                 x1[:, q, :], ALU.mult, ALU.add)
                link(ins)
                dve.wait_ge(h_saved, a + 1)
                d.tensor_tensor(h1[:, qs[0]:qs[-1] + 1, :], h1[:, qs[0]:qs[-1] + 1, :],
                                x1[:, qs[0]:qs[-1] + 1, :], ALU.add).then_inc(attended, 1)
                link.end()
                if gi < 3:
                    dve.wait_ge(attended, 4 * a + gi + 1)
                    for q in qs:
                        ins = d.bn_stats(st2[:, q, :], h1[:, q, :])
                    ins.then_inc(st2_done, 1)

            def router_logits(f):
                dve.wait_ge(logits, f + 1)
                link = Link(dve, ch_fin, f * N_FIN, N_FIN)
                dve.wait_ge(ld, 16 * 4)
                link(d.tensor_tensor(lg[:], psO[:, 0:T * E].rearrange("p (t e) -> p t e", e=E),
                                     rb[:].unsqueeze(1).broadcast_to([P, T, E]), ALU.add))
                link(d.tensor_reduce(r6[:, 0, :], lg[:], AX.X, ALU.max))
                d.tensor_tensor(lg[:], lg[:], r6[:, 0, :].unsqueeze(2).broadcast_to([P, T, E]),
                                ALU.subtract).then_inc(lg_ready, 1)
                return link

            def wide(x):
                return x.unsqueeze(2).broadcast_to([P, T, E])

            def router_probs(f, link):
                dve.wait_ge(pr_ready, f + 1)
                link(d.tensor_reduce(r6[:, 1, :], pr[:], AX.X, ALU.add))
                link(d.reciprocal(r6[:, 2, :], r6[:, 1, :]))
                link(d.tensor_tensor(pr[:], pr[:], wide(r6[:, 2, :]), ALU.mult))

            def choose(link, n):
                left = (pr, lg)[n][:]
                link(d.tensor_reduce(r6[:, 3 + n, :], left, AX.X, ALU.max))
                link(d.tensor_tensor(sel[:, 0, :, :], left, wide(r6[:, 3 + n, :]), ALU.is_lt))
                link(d.scalar_tensor_tensor(sel[:, 0, :, :], sel[:, 0, :, :], float(E), iota16[:],
                                            ALU.mult, ALU.add))
                link(d.tensor_reduce(r6[:, 5 + n, :], sel[:, 0, :, :], AX.X, ALU.min))
                link(d.tensor_tensor(sel[:, 1 + n, :, :], iota16[:], wide(r6[:, 5 + n, :]), ALU.is_equal))
                if n == 0:
                    link(d.scalar_tensor_tensor(lg[:], sel[:, 1, :, :], -2.0, pr[:], ALU.mult, ALU.add))

            def choices(link):
                choose(link, 1)
                link(d.tensor_tensor(mask[:], sel[:, 1, :, :], sel[:, 2, :, :], ALU.add))
                d.tensor_scalar(mask[:, T - 1, :], mask[:, T - 1, :], valid[:], None, ALU.mult).then_inc(mask_ready, 1)
                link.end()

            def ranks(f):
                dve.wait_ge(rank_psum, f + 1)
                dve.wait_ge(mask_ready, f + 1)
                d.tensor_tensor(tpos[:], psO[:, 0:T * E].rearrange("p (t e) -> p t e", e=E), eoff[:], ALU.add)\
                    .then_inc(rank_read, 1)

            def positions(f):
                link = Link(dve, ch_pos, f * N_POS, N_POS)
                d.tensor_reduce(cnt[:, 1, :], mask[:].rearrange("p t e -> p e t"), AX.X, ALU.add)
                dve.wait_ge(rank_read, f + 1)
                for k in range(2):
                    link(d.tensor_tensor(sel[:, 0, :, :], sel[:, 1 + k, :, :], tpos[:], ALU.mult))
                    link(d.tensor_reduce(pos[:, k, :], sel[:, 0, :, :], AX.X, ALU.add))
                last = pos[:, :, T - 1]
                link(d.tensor_scalar(last, last, valid[:], None, ALU.mult))
                link(d.tensor_tensor(last, last, spill[:], ALU.add))
                after(dve, scattered, 16 * 2 * T * f)
                d.tensor_scalar(posu[:], pos[:], 1.0, None, ALU.mult)
                link(d.tensor_scalar(spill[:], spill[:], invalid[:], None, ALU.add))
                d.tensor_copy(xrow[:, :, D], r6[:, 5, :])
                d.tensor_copy(xrow[:, :, D + 1:D + 3], r6[:, 3:5, :].rearrange("p a t -> p t a"))
                link(d.tensor_copy(xrow[:, :, D + 3], dest[:]))
                d.tensor_tensor(cnt[:, 0, :], cnt[:, 0, :], cnt[:, 1, :], ALU.add)
                link(d.tensor_scalar(dest[:], dest[:], float(STEPS), None, ALU.add))
                link.end()
                d.tensor_copy(pos[:, 0, 0:1], pos[:, 0, 0:1]).then_inc(pos_ready, 1)

            def body(b, tok, att, fin):
                a, f = b - 1, b - 2
                if tok:
                    after(dve, loc3_ready, T * b + 2)
                    after(dve, dy_ready, T * b)
                    d.tensor_copy(v_cur[:], v_nxt[:]).then_inc(v_cur_ready, 1)
                    dve.wait_ge(v_cur_ready, b + 1)
                if att:
                    var1_of(a)
                if fin:
                    x2_of(f)
                link = None
                for i in range(T):
                    if tok:
                        if i + 1 < T:
                            lo_of(b, i + 1)
                    if att and i == 0:
                        x1_of(a)
                    if tok:
                        if i + 2 < T:
                            inc3_of(b, i + 2, v_cur)
                        if i >= 2:
                            dve.wait_ge(h_ready, T * b + i - 1)
                            d.bn_stats(st1[:, i - 2, :], hb[:, i - 2, :]).then_inc(st1_done, 1)
                        if i == 2:
                            inc2_of(b + 1)
                        if i == T - 1:
                            a2_of(b + 1)
                            inc3_of(b + 1, 0, v_nxt)
                            packs_of(b + 1)
                            inc3_of(b + 1, 1, v_nxt)
                    if fin and i == 1:
                        router_probs(f, link)
                    if tok:
                        weigh(b, i, 0)
                    if fin and i == 1:
                        choose(link, 0)
                    if att and i == 1:
                        k_copy(a)
                    if fin and i == 1:
                        choices(link)
                    if fin and i == 2:
                        ranks(f)
                    if fin and i == 3:
                        positions(f)
                    if tok:
                        weigh(b, i, 1)
                    if fin and i == 0:
                        link = router_logits(f)
                    if att and i >= 1:
                        if 2 <= i < T - 1:
                            attend(a, i - 2)
                        if i - 1 < 4:
                            negmax_of(a, i - 1)
                if tok:
                    lo_of(b + 1, 0)
                if att:
                    attend(a, len(GROUPS) - 1)
                    var2_of(a)

            inc2_of(0)
            a2_of(0)
            inc3_of(0, 0, v_nxt)
            packs_of(0)
            inc3_of(0, 1, v_nxt)
            lo_of(0, 0)
            for k in range(6):
                dve.wait_ge(w_hi, k + 1)
                d.tensor_tensor(w4l[:, k, :], wstage[k], w4h[:, k, :].bitcast(F32),
                                ALU.subtract).then_inc(w_split, 1)
            dve.wait_ge(w_split, 6)
            d.tensor_copy(w4l[64:96, 5, :], w4h[64:96, 5, :].bitcast(F32)).then_inc(w_split, 1)

            body(0, True, False, False)
            body(1, True, True, False)
            with dve.Fori(2, B) as b:
                body(b, True, True, True)
            body(B, False, True, True)
            x2_of(B - 1)
            last = router_logits(B - 1)
            router_probs(B - 1, last)
            choose(last, 0)
            choices(last)
            ranks(B - 1)
            positions(B - 1)

            link = Link(dve, ch_tab, 0, 12)
            dve.wait_ge(counts, 1)
            link(d.tensor_scalar(tiles_i[0:E, :], psO[0:E, 0:1], 1.0 / SLOT, (SLOT - 1) / SLOT - 0.5 + 0.5 / SLOT,
                                 ALU.mult, ALU.add))
            d.tensor_copy(tiles_f[0:E, 0:1], tiles_i[0:E, :]).then_inc(tiles_ready, 1)
            link(d.tensor_tensor(fillrow[:], psS[:, 0:E], eoff[:, 0, :], ALU.add))
            dve.wait_ge(tiles_sum, 1)
            link(d.tensor_copy(tiles_f[0:E, 1:2], psO[0:E, 16:17]))
            link(d.tensor_scalar(ind[0:E, 0, :], iotaj[0:E, :], tiles_f[0:E, 1:2], None, ALU.is_ge))
            d.tensor_scalar(ind[0:E, 1, :], ind[0:E, 0, :], tiles_f[0:E, 0:1], None, ALU.mult).then_inc(ind_ready, 1)
            dve.wait_ge(slot_sum, 1)
            link(d.scalar_tensor_tensor(slot_f[:, 1, :], psS[:, SLOTX:2 * SLOTX], -1.0, iotaj[:], ALU.mult, ALU.add))
            link(d.tensor_scalar(slot_f[:, 0, :], psS[:, 0:SLOTX], float(REGION / SLOT), None, ALU.mult))
            link(d.tensor_tensor(slot_f[:, 1, :], slot_f[:, 1, :], slot_f[:, 0, :], ALU.add))
            d.tensor_scalar(slot_i[:, 1, :], slot_f[:, 1, :], float(SLOT), float(DUMMY), ALU.mult, ALU.min)
            link(d.scalar_tensor_tensor(slot_f[:, 2, :], psS[:, 0:SLOTX], float(E), iotaj[:], ALU.is_equal, ALU.mult))
            link(d.tensor_tensor(slot_f[:, 2, :], slot_f[:, 2, :], psS[:, SLOTX:2 * SLOTX], ALU.max))
            link(d.tensor_scalar(slot_f[:, 0, :], psS[:, 0:SLOTX], float(E - 1), None, ALU.min))
            for k in range(RING):
                ins = d.tensor_scalar(seen_i[:, k, :], slot_f[:, 2, :], float(RING - 1 - k), 32.0 / RING, ALU.add, ALU.mult)
            link(ins)
            link(d.tensor_scalar(seen_i[:], seen_i[:], -32, 16, ALU.bitwise_and, ALU.bitwise_or))
            link.end()
            d.tensor_copy(slot_i[:, 0, :], slot_f[:, 0, :]).then_inc(table, 1)
            dve.wait_ge(table, 1)

            def w1_of(j, u, k, ex):
                after(dve, up, 2 * j - 2)
                after(dve, gelu, j - 1)
                w1e = w1_all[:, bass.ds(ex, 1), :].rearrange("p a f -> p (a f)")
                d.tensor_scalar(w1h[:, u, :], w1e, 1.0, None, ALU.mult).then_inc(w1_hi, 1)
                d.tensor_scalar(biasc[:, k, :], biases[:, bass.ds(ex, 1), :].rearrange("p a c -> p (a c)"), 1.0, None, ALU.mult)
                dve.wait_ge(w1_hi, j + 1)
                d.tensor_tensor(w1l[:, u, :], w1e, w1h[:, u, :].bitcast(F32), ALU.subtract).then_inc(w1_ready, 1)

            def xT_lower(j, u):
                dve.wait_ge(xT_hi, j + 1)
                d.tensor_tensor(xTl[:, u, :], psX[:, 0:SLOT], xTh[:, u, :].bitcast(F32), ALU.subtract)\
                    .then_inc(xT_ready, 1)

            def meta_of(j, u, k, n):
                rows = xg[:, k, :].rearrange("p (s c) -> p s c", s=2)
                ev = slot_f[:, 0, j:j + 1] if isinstance(j, int) else slot_f[:, 0, bass.ds(j, 1)]
                if not isinstance(n, int) or n > 0:
                    dve.wait_ge(added[k], 16 + 32 * n)
                after(dve, y_ready, j - 1)
                link = Link(dve, ch_meta, j, 1)
                d.scalar_tensor_tensor(gtmp[:, u, 0, :], rows[:, :, D], ev, rows[:, :, D + 1], ALU.is_equal, ALU.mult)
                link(d.scalar_tensor_tensor(gtmp[:, u, 1, :], rows[:, :, D], ev, rows[:, :, D + 2], ALU.not_equal, ALU.mult))
                d.tensor_copy(destu[:, k, :], rows[:, :, D + 3])
                d.tensor_tensor(gate[:, u, :], gtmp[:, u, 0, :], gtmp[:, u, 1, :], ALU.add).then_inc(meta_ready, 1)
                link.end()

            def y_of(j, u, k):
                dve.wait_ge(down, j + 1)
                b2e = biasc[:, k, FF // P:].unsqueeze(1).broadcast_to([P, 2, D])
                d.tensor_tensor(yr[:, k, :].rearrange("p (s d) -> p s d", s=2),
                                psY[u].rearrange("p (s d) -> p s d", s=2), b2e, ALU.add).then_inc(y_sum, 1)

            def expert_of(j):
                return dve.value_load(slot_i[0:1, 0, j:j + 1] if isinstance(j, int) else slot_i[0:1, 0, bass.ds(j, 1)],
                                      min_val=0, max_val=E - 1)

            def slot(j, u, k, n):
                w1_of(j + 1, 1 - u, (k + 1) % RING, expert_of(j + 1))
                xT_lower(j + 1, 1 - u)
                dve.wait_ge(xg_in[k], 16 * (n + 1))
                meta_of(j, u, k, n)
                if not isinstance(j, int) or j > 0:
                    y_of(j - 1, 1 - u, (k - 1) % RING)

            dve.wait_ge(wl, 16)
            dve.wait_ge(wl2, 48)
            w1_of(0, 0, 0, expert_of(0))
            xT_lower(0, 0)
            for j in range(PEEL):
                slot(j, j % 2, j % RING, j // RING)
            with dve.Fori(0, (SLOTS - PEEL) // RING) as n:
                for k in range(PEEL, PEEL + RING):
                    slot(n * RING + k, k % 2, k % RING, n + k // RING)
            y_of(SLOTS - 1, (SLOTS - 1) % 2, (SLOTS - 1) % RING)

        @block.tensor
        def _(pe):
            t_ = nc.tensor
            pe.wait_ge(consts, N_CONST)

            def s2_of(b):
                pe.wait_ge(inc2_ready, b + 1)
                pe.wait_ge(run2_ready, b + 1)
                after(pe, h_ready, T * (b - 1) + 4)
                o = psS[:, 0:T * 64]
                t_.matmul(o, before[:, 0:P], inc2[:].rearrange("p t n -> p (t n)"), start=True, stop=False)
                t_.matmul(o, ones[:], run2[:].rearrange("p t n -> p (t n)"), start=False, stop=True)\
                    .then_inc(s2_sum, 1)

            def a3_of(b, i):
                pe.wait_ge(inc3_ready, T * b + i + 1)
                pe.wait_ge(loc3_ready, T * b + i + 1)
                after(pe, a3_lo, 2 * T * b + 2 * i)
                for k in range(4):
                    o = psA[:, k // 2, (k % 2) * 129:(k % 2) * 129 + 129]
                    t_.matmul(o, inc3[:, i % 2, k * P:(k + 1) * P], before[:], start=True, stop=False)
                    ins = t_.matmul(o[:, 0:P], loc3[:, i % 2, k * P:(k + 1) * P], ident[:], is_transpose=True,
                                    start=False, stop=True)
                    if k % 2:
                        ins.then_inc(a3_sum, 1)

            def pack_of(b, i):
                pe.wait_ge(a2_ready, b + 1)
                after(pe, h_ready, T * b + (-1, 0, 0, 1, 2, 3)[i])
                after(pe, pack_copied, T * b + i)
                t_.transpose(psS[:, 0:P], pack[:, i, 0:P], ident[:])
                t_.transpose(psS[:, P:2 * P], pack[:, i, P:2 * P], ident[:]).then_inc(pack_sum, 1)

            def main_of(b, i, h):
                after(pe, weighed, LH * (2 * T * b + 2 * i + h - 1))
                if h == 0:
                    pe.wait_ge(a3_lo, 2 * T * b + 2 * i + 2)
                    pe.wait_ge(pack_copied, T * b + i + 1)
                o = psP[:, h, :]
                cols = slice(h * 512, h * 512 + 512)
                first = True
                start = isinstance(b, int) and T * b + i + h == 0
                for k in range(4):
                    if start:
                        pe.wait_ge(w_split, k + 1)
                    hi, lo = (x[:, i % 2, k * P:(k + 1) * P] for x in (a3h, a3l))
                    for left, right in ((lo, w4h), (hi, w4l), (hi, w4h)):
                        t_.matmul(o, left, right[:, k, cols], start=first, stop=False)
                        first = False
                if start:
                    pe.wait_ge(w_split, 7)
                t_.matmul(o, packT[:, i % 2, P:2 * P], w4l[:, 5, cols], start=False, stop=False)
                t_.matmul(o, packT[:, i % 2, 0:P], w4h[:, 4, cols], start=False, stop=True)\
                    .then_inc(main_done, 1)

            def path_of(b, i):
                pe.wait_ge(dy_ready, T * b + i + 1)
                if i >= 1:
                    pe.wait_ge(h_ready, T * b + i)
                if i <= 3:
                    pe.wait_ge(pack_copied, T * b + i + 3)
                elif i == 4:
                    pe.wait_ge(s2_read, b + 2)
                else:
                    pe.wait_ge(pack_copied, T * (b + 1) + 1)
                o = psS[:, 0:P]
                t_.matmul(o, upto[:], dy[:, i % 2, :], start=True, stop=False)
                left, right = (ones[:], bias0[:]) if i == 0 else (last_row[:], hb[:, i - 1, :])
                t_.matmul(o, left, right, start=False, stop=True).then_inc(path_sum, 1)

            def x1T_of(a):
                pe.wait_ge(x1_ready, a + 1)
                pe.wait_ge(x1_upper, a + 1)
                for i in range(T):
                    if i in (0, 4):
                        after(pe, x2T_ready, 2 * a - 1 + i // 4)
                    ins = t_.transpose(psW[:, i * P:(i + 1) * P], x1[:, i, :], ident[:])
                ins.then_inc(x1T_psum, 1)

            def k_of(a):
                pe.wait_ge(x1T_ready, a + 1)
                after(pe, lg_ready, a)
                t_.matmul(psW[:, 0:512], waT[:], x1T[:, 0:512], start=True, stop=True)
                t_.matmul(psW[:, 512:768], waT[:], x1T[:, 512:768], start=True, stop=True)
                for i in range(T):
                    o = psO[:, i * D:(i + 1) * D] if i < 4 else psW[:, (i + 2) * D:(i + 3) * D]
                    ins = t_.matmul(o, x1T[:, i * P:(i + 1) * P], waT[:], start=True, stop=True)
                ins.then_inc(k_psum, 1)

            def scores_of(a, gi):
                if gi == 0:
                    pe.wait_ge(k_ready, a + 1)
                    pe.wait_ge(k_ready2, a + 1)
                else:
                    pe.wait_ge(pT_ready, 4 * a + gi)
                for q in GROUPS[gi]:
                    base, n = PLACE[q], q * P
                    left = x1T[:, q * P:(q + 1) * P]
                    for c0 in range(0, n, 512):
                        c1 = min(c0 + 512, n)
                        t_.matmul(psW[:, base + c0:base + c1], left, kT[:, c0:c1], start=True, stop=True)
                    o = psW[:, base + n:base + n + P]
                    t_.matmul(o, left, kT[:, n:n + P], start=True, stop=False)
                    ins = t_.matmul(o, ident16[:], future[:], start=False, stop=True)
                ins.then_inc(scores, 1)

            def pT_of(a, gi):
                pe.wait_ge(exp_ready, 4 * a + gi + 1)
                for q in GROUPS[gi]:
                    for k in range(q + 1):
                        c = PLACE[q] + k * P
                        ins = t_.transpose(psW[:, c:c + P], probs[:, c:c + P], ident[:])
                ins.then_inc(pT_psum, 1)

            def pv_of(a, gi):
                pe.wait_ge(pT_ready, 4 * a + gi + 1)
                if gi == 0:
                    pe.wait_ge(k_ready2, a + 1)
                    after(pe, rank_read, a)
                else:
                    pe.wait_ge(attended, 4 * a + gi)
                for s, q in enumerate(GROUPS[gi]):
                    for k in range(q + 1):
                        c = PLACE[q] + k * P
                        ins = t_.matmul(psO[:, s * D:(s + 1) * D], probsT[:, c:c + P], kk[:, k, :],
                                        start=(k == 0), stop=(k == q))
                ins.then_inc(pv_psum, 1)

            def x2T_of(f):
                pe.wait_ge(x2_ready, f + 1)
                pe.wait_ge(x2_upper, f + 1)
                for i in range(T):
                    ins = t_.transpose(psW[:, i * P:(i + 1) * P], x2[:, i, :], ident[:])
                    if i in (3, T - 1):
                        ins.then_inc(x2T_psum, 1)

            def logits_of(f):
                pe.wait_ge(x2T_ready, 2 * f + 2)
                pe.wait_ge(attended, 4 * f + 4)
                for i in range(T):
                    ins = t_.matmul(psO[:, i * E:(i + 1) * E], x2T[:, i * P:(i + 1) * P], rwT[:],
                                    start=True, stop=True)
                ins.then_inc(logits, 1)

            def rank_of(f):
                pe.wait_ge(mask_ready, f + 1)
                o = psO[:, 0:T * E]
                t_.matmul(o, before[:, 0:P], mask[:].rearrange("p t e -> p (t e)"), start=True, stop=False)
                for i in range(T - 1):
                    t_.matmul(psO[:, (i + 1) * E:T * E], ones[:],
                              mask[:, i, :].unsqueeze(1).broadcast_to([P, T - 1 - i, E]), start=False, stop=False)
                t_.matmul(o, ones[:], cnt[:, 0, :].unsqueeze(1).broadcast_to([P, T, E]), start=False, stop=True)\
                    .then_inc(rank_psum, 1)

            def body(b, tok, att, fin):
                a, f = b - 1, b - 2
                if att:
                    path_of(a, T - 1)
                for i in range(T):
                    if tok:
                        if i + 1 < T:
                            pack_of(b, i + 1)
                            a3_of(b, i + 1)
                        else:
                            s2_of(b + 1)
                        main_of(b, i, 0)
                        if i >= 1:
                            path_of(b, i - 1)
                    if att:
                        if i == 1:
                            k_of(a)
                        if i >= 2:
                            pT_of(a, i - 2)
                    if fin and i == 2:
                        rank_of(f)
                    if tok:
                        main_of(b, i, 1)
                    if fin and i == 0:
                        x2T_of(f)
                    if att and i == 0:
                        x1T_of(a)
                    if fin and i == 0:
                        logits_of(f)
                    if att:
                        if 2 <= i < T - 1:
                            pv_of(a, i - 2)
                        if 1 <= i < 5:
                            scores_of(a, i - 1)
                if tok:
                    pack_of(b + 1, 0)
                    a3_of(b + 1, 0)
                if att:
                    pv_of(a, len(GROUPS) - 1)

            pe.wait_ge(ld, 16 * 4)
            s2_of(0)
            pack_of(0, 0)
            a3_of(0, 0)
            body(0, True, False, False)
            body(1, True, True, False)
            with pe.Fori(2, B) as b:
                body(b, True, True, True)
            body(B, False, True, True)
            x2T_of(B - 1)
            logits_of(B - 1)

            rank_of(B - 1)
            pe.wait_ge(pos_ready, B)
            t_.matmul(psS[:, 0:E], ones[:], cnt[:, 0, :], start=True, stop=True)
            t_.matmul(psO[0:E, 0:1], cnt[:, 0, :], ones[:, 0:1], start=True, stop=True).then_inc(counts, 1)
            pe.wait_ge(tiles_ready, 1)
            t_.matmul(psO[0:E, 16:17], upto[0:E, 0:E], tiles_f[0:E, 0:1], start=True, stop=True).then_inc(tiles_sum, 1)
            pe.wait_ge(ind_ready, 1)
            t_.matmul(psS[:, 0:2 * SLOTX], ones[0:E, :], ind[0:E, :, :].rearrange("p a j -> p (a j)"),
                      start=True, stop=True).then_inc(slot_sum, 1)

            def xT_of(j, u, k, n):
                pe.wait_ge(xg_in[k], 16 * (n + 1))
                after(pe, xT_ready, j)
                for s in range(2):
                    ins = t_.transpose(psX[:, s * P:(s + 1) * P], xg[:, k, s * ROW:s * ROW + D], ident[:])
                ins.then_inc(xT_psum, 1)

            def up_of(j, u):
                pe.wait_ge(xT_ready, j + 1)
                pe.wait_ge(w1_ready, j + 1)
                after(pe, gelu, j - 1)
                for c in range(4):
                    wh, wl_ = (w[:, u, c * P:(c + 1) * P] for w in (w1h, w1l))
                    for left, right in ((wl_, xTh), (wh, xTl), (wh, xTh)):
                        ins = t_.matmul(psH[u][:, c * SLOT:(c + 1) * SLOT], left, right[:, u, :],
                                        start=(left is wl_), stop=(right is xTh and left is wh))
                    if c % 2:
                        ins.then_inc(up, 1)

            def down_of(j, u, ex):
                pe.wait_ge(gelu, j + 1)
                after(pe, y_sum, j - 1)
                for s in range(2):
                    for c in range(4):
                        ins = t_.matmul(psY[u][:, s * D:(s + 1) * D], hTc[:, u, c, s * P:(s + 1) * P],
                                        w2_all[:, bass.ds(ex * 4 + c, 1), :].rearrange("p a d -> p (a d)"),
                                        start=(c == 0), stop=(c == 3))
                ins.then_inc(down, 1)

            def expert_of(j):
                return pe.value_load(slot_i[0:1, 0, j:j + 1] if isinstance(j, int) else slot_i[0:1, 0, bass.ds(j, 1)],
                                     min_val=0, max_val=E - 1)

            def slot(j, u, k1, n1):
                up_of(j, u)
                xT_of(j + 1, 1 - u, k1, n1)
                if not isinstance(j, int) or j > 0:
                    down_of(j - 1, 1 - u, expert_of(j - 1))

            pe.wait_ge(table, 1)
            pe.wait_ge(wl2, 48)
            xT_of(0, 0, 0, 0)
            for j in range(PEEL):
                slot(j, j % 2, (j + 1) % RING, (j + 1) // RING)
            with pe.Fori(0, (SLOTS - PEEL) // RING) as n:
                for k in range(PEEL, PEEL + RING):
                    slot(n * RING + k, k % 2, (k + 1) % RING, n + (k + 1) // RING)
            down_of(SLOTS - 1, (SLOTS - 1) % 2, expert_of(SLOTS - 1))


def kernel(x, L0_tok_W, L0_tok_b, L0_attn_W, L0_ffn_router_w, L0_ffn_router_b, L0_ffn_w1, L0_ffn_b1,
           L0_ffn_w2, L0_ffn_b2):
    import numpy as np
    import concourse.bacc as bacc
    from concourse.bass_utils import run_bass_kernel_spmd

    f32 = np.float32
    x = np.asarray(x)
    n = STEPS + 1
    time = np.arange(n, dtype=f32) * f32(1.0 / STEPS)
    time[-1] = 1.0
    path = np.concatenate([np.broadcast_to(time[:, None, None], (n, B, 1)), x.transpose(1, 0, 2)], axis=2)
    path = np.pad(path, ((0, T * P + 1 - n), (0, 0), (0, 0)), mode="edge")

    def tiles(a):
        return np.ascontiguousarray(a.reshape(T, P, B, C).transpose(1, 2, 0, 3).reshape(P, B * T * C))

    W = np.asarray(L0_tok_W)
    W1t, W2t, W3t, W4t = (W[:, lo:lo + C ** k].T.reshape(-1, C * D)
                          for k, lo in ((1, 0), (2, C), (3, C + C ** 2), (4, C + C ** 2 + C ** 3)))
    gap = np.zeros((15, C * D), f32)
    w3y = np.concatenate([W3t, W2t, W2t, W1t, gap, W2t, W1t, np.zeros((23, C * D), f32)])
    w1 = np.asarray(L0_ffn_w1).transpose(0, 2, 1)
    w2 = np.asarray(L0_ffn_w2).transpose(0, 2, 1).reshape(E, FF // P, P, D).transpose(0, 2, 1, 3)
    arrays = {
        "xa": tiles(path[:-1]), "xb": tiles(path[1:]), "x0": path[0].reshape(1, B * C),
        "w4": W4t, "w3x": np.concatenate([W3t, W3t]), "w3y": w3y, "tok_b": np.asarray(L0_tok_b)[None],
        "attn_w": np.asarray(L0_attn_W).T, "router_w": np.asarray(L0_ffn_router_w).T,
        "router_b": np.asarray(L0_ffn_router_b)[None],
        "w1": w1, "b1": np.asarray(L0_ffn_b1).reshape(E, FF // P, P).transpose(0, 2, 1),
        "w2": w2, "b2": np.asarray(L0_ffn_b2),
    }
    arrays = {k: np.ascontiguousarray(a) for k, a in arrays.items()}
    nc = bacc.Bacc("TRN2", target_bir_lowering=False, num_devices=1)
    aps = {k: nc.dram_tensor(k, a.shape, mybir.dt.from_np(a.dtype), kind="ExternalInput").ap()
           for k, a in arrays.items()}
    out = nc.dram_tensor("out", (OUT_ROWS + SLOT, D), F32, kind="ExternalOutput").ap()
    build(nc, out=out, **aps)
    return run_bass_kernel_spmd(nc, [arrays], core_ids=[0]).results[0]["out"][:OUT_ROWS].reshape(B, STEPS, D)
```
